# Optimizing a Trainium2 kernel written in Bass

```python
import numpy as np
import jax
import jax.numpy as jnp

def _softmax(x, axis=-1):
    return jax.nn.softmax(x, axis=axis)

def _gelu(x):
    return jax.nn.gelu(x, approximate=True)

def _silu(x):
    return jax.nn.silu(x)

def _sigmoid(x):
    return jax.nn.sigmoid(x)

def _layernorm(x, axis=-1, eps=1e-05):
    m = jnp.mean(x, axis=axis, keepdims=True)
    v = jnp.var(x, axis=axis, keepdims=True)
    return (x - m) / jnp.sqrt(v + eps)

def _scatter_add(tgt, idx, src, axis=0):
    return tgt.at[idx].add(src)

def _segment_sum(src, seg, n):
    return jax.ops.segment_sum(src, seg, n)
kernel_name = 'mk_gnn_resnorm_d1_gnn_r32_bc9e4c'

def setup_inputs(seed: int=0):
    np.random.seed(seed)
    _w = jnp.asarray

    def _rec_inputs():
        import jax
        import jax.numpy as jnp
        _gk = jax.random.key(seed)
        x = -2.02e-05 + 0.1 * jax.random.normal(jax.random.fold_in(_gk, 1), (50000, 64), jnp.float32)
        src = jax.random.randint(jax.random.fold_in(_gk, 2), (50000,), 0, 50000, jnp.int32)
        dst = jnp.minimum((50000 * jax.random.uniform(jax.random.fold_in(_gk, 3), (50000,)) ** 2.0).astype(jnp.int32), 49999)
        _o = jnp.argsort(dst, stable=True)
        src = src[_o]
        dst = dst[_o]
        edge_type_20 = jax.random.randint(jax.random.fold_in(_gk, 12), (50000,), 0, 20, jnp.int32)
        return (x, src, dst, edge_type_20)
    x, src, dst, edge_type_20 = _rec_inputs()

    def _L0_gnn_setup():
        import jax, jax.numpy as jnp
        import numpy as np
        N_ENT = 3125
        N_REL = 20
        N_EDGE = 31250
        C = 64
        N_HOPS = 2
        EPS = 1e-12

        def _agg(ent, rel, head, tail, etype, fc_w, fc_b):
            n = ent.shape[0]
            a_input = jnp.concatenate([ent[head], ent[tail]], axis=-1)
            e_input = jnp.sum((a_input @ fc_w.T + fc_b) * rel[etype], axis=-1)
            e = jax.nn.leaky_relu(e_input, negative_slope=0.2)
            m = jax.ops.segment_max(e, head, num_segments=n)
            exp_e = jnp.exp(e - m[head])
            denom = jax.ops.segment_sum(exp_e, head, num_segments=n)
            alpha = exp_e / denom[head]
            agg = jax.ops.segment_sum(ent[tail] * alpha[:, None], head, num_segments=n)
            return agg + ent
        key = jax.random.key(seed)
        k1, k2, k3, k4, k5 = jax.random.split(key, 5)
        entity_emb = jax.random.normal(k1, (N_ENT, C), dtype=jnp.float32) * 0.1
        relation_emb = jax.random.normal(k2, (N_REL, C), dtype=jnp.float32) * 0.1
        edge_index = jax.random.randint(k3, (2, N_EDGE), 0, N_ENT, dtype=jnp.int64)
        edge_type = jax.random.randint(k4, (N_EDGE,), 0, N_REL, dtype=jnp.int64)
        fc_w = jax.random.normal(k5, (C, 2 * C), dtype=jnp.float32) * (1.0 / np.sqrt(2 * C))
        fc_b = jnp.zeros((C,), dtype=jnp.float32)
        return {'entity_emb': entity_emb, 'relation_emb': relation_emb, 'edge_index': edge_index, 'edge_type': edge_type, 'fc_w': fc_w, 'fc_b': fc_b}
    _L0_gnn_all = _L0_gnn_setup()
    _L0_gnn_in = {k: v for k, v in _L0_gnn_all.items() if k in ('relation_emb', 'fc_w', 'fc_b')}
    del _L0_gnn_all
    return {'x': x, 'src': src, 'dst': dst, 'edge_type_20': edge_type_20, 'L0_gnn_relation_emb': _L0_gnn_in['relation_emb'], 'L0_gnn_fc_w': _L0_gnn_in['fc_w'], 'L0_gnn_fc_b': _L0_gnn_in['fc_b']}

def reference(x, src, dst, edge_type_20, L0_gnn_relation_emb, L0_gnn_fc_w, L0_gnn_fc_b):
    import jax
    import jax.numpy as jnp

    def _L0_gnn_ref(entity_emb, relation_emb, edge_index, edge_type, fc_w, fc_b):
        import jax, jax.numpy as jnp
        import numpy as np
        N_ENT = 3125
        N_REL = 20
        N_EDGE = 31250
        C = 64
        N_HOPS = 2
        EPS = 1e-12

        def _agg(ent, rel, head, tail, etype, fc_w, fc_b):
            n = ent.shape[0]
            a_input = jnp.concatenate([ent[head], ent[tail]], axis=-1)
            e_input = jnp.sum((a_input @ fc_w.T + fc_b) * rel[etype], axis=-1)
            e = jax.nn.leaky_relu(e_input, negative_slope=0.2)
            m = jax.ops.segment_max(e, head, num_segments=n)
            exp_e = jnp.exp(e - m[head])
            denom = jax.ops.segment_sum(exp_e, head, num_segments=n)
            alpha = exp_e / denom[head]
            agg = jax.ops.segment_sum(ent[tail] * alpha[:, None], head, num_segments=n)
            return agg + ent
        head, tail = (edge_index[0], edge_index[1])
        ent = entity_emb
        for _ in range(N_HOPS):
            ent = _agg(ent, relation_emb, head, tail, edge_type, fc_w, fc_b)
            norm = jnp.linalg.norm(ent, axis=-1, keepdims=True)
            ent = ent / jnp.maximum(norm, EPS)
        return ent
    edge_index = jnp.stack([src, dst])
    x = _layernorm(x + _L0_gnn_ref(x, L0_gnn_relation_emb, edge_index, edge_type_20, L0_gnn_fc_w, L0_gnn_fc_b), axis=-1)
    return x

_drawn_inputs = setup_inputs


def setup_inputs(seed=0):
    import zlib

    import numpy as np

    out = dict(_drawn_inputs(seed))
    spreads = {'L0_gnn_fc_b': (0.0, 0.8)}
    factors = {'L0_gnn_relation_emb': 3.756, 'L0_gnn_fc_w': 4.319}
    for name, (base, spread) in spreads.items():
        noise = np.random.default_rng([zlib.crc32(name.encode()), seed]).standard_normal(out[name].shape)
        drawn = base * np.exp(spread * noise) if base else spread * noise
        out[name] = jnp.asarray(drawn.astype(out[name].dtype))
    for name, factor in factors.items():
        out[name] = (out[name] * factor).astype(out[name].dtype)
    return out
```

```python
from contextlib import ExitStack

import concourse.bass as bass
from concourse import mybir

F32, BF16, I32, U32 = mybir.dt.float32, mybir.dt.bfloat16, mybir.dt.int32, mybir.dt.uint32
ALU = mybir.AluOpType
ACT = mybir.ActivationFunctionType
AX = mybir.AxisListType

P = 128
BIG = 1.0e30
FAR = 4.0e6


class Link:

    def __init__(self, eng, sem):
        self.eng, self.sem, self.base, self.n = eng, sem, 0, 0

    def enter(self, i, per):
        self.i, self.per, self.n = i, per, 0

    def plain(self):
        self.i, self.per, self.n = 0, 0, 0

    def leave(self, steps):
        assert self.per == 0 or self.n == self.per, (self.n, self.per)
        self.base += steps * self.n
        self.plain()

    def __call__(self, ins):
        ins.then_inc(self.sem, 1)
        self.n += 1
        self.eng.wait_ge(self.sem, self.base + self.n + self.i * self.per)


def build_gnn(nc, x, src, dst, etype, rel, fc_w, fc_b, out):
    N, C = x.shape
    E = src.shape[0]
    R = rel.shape[0]
    K = 14
    T = 2 * K * -(-max(N, E) // (P * 2 * K))
    NCH = T // K
    NPAD = P * T
    HI = NPAD // P
    CO = C + 1
    A0, B0, X0 = CO, CO + R, CO + 2 * R
    W0 = X0
    W1 = X0 + C
    full, rest = (N // T, N % T)
    assert E == N and HI <= 512 and full == P - 1

    table0 = nc.dram_tensor("table0", [NPAD, W0], F32, kind="Internal").ap()
    table1 = nc.dram_tensor("table1", [NPAD, W1], F32, kind="Internal").ap()
    by_lo = nc.dram_tensor("by_lo", [NPAD, 4], I32, kind="Internal").ap()
    by_head = nc.dram_tensor("by_head", [NPAD + 1, 4], I32, kind="Internal").ap()

    ctx = ExitStack()
    with ctx:
        def sb(name, shape, dt=F32):
            return ctx.enter_context(nc.sbuf_tensor(name, shape, dt))

        def pb(name, shape, dt=F32):
            return ctx.enter_context(nc.psum_tensor(name, shape, dt))

        def sem(name):
            return ctx.enter_context(nc.semaphore(name))

        iota_i = sb("iota_i", [P, HI], I32)
        iota_f = sb("iota_f", [P, HI])
        iota_r = sb("iota_r", [P, R])
        ident = sb("ident", [P, P])
        ident_b = sb("ident_b", [P, P], BF16)
        ones = sb("ones", [P, P])
        before = sb("before", [P, P])
        after = sb("after", [P, P])
        zeros = sb("zeros", [P, HI])
        w_sb = sb("w_sb", [C, 2 * C])
        relT = sb("relT", [C, R])
        bias_c = sb("bias_c", [C, 1])
        bias_rep = sb("bias_rep", [C, P])
        V = sb("V", [C, 2 * R])
        brel = sb("brel", [P, R])
        raw = sb("raw", [P, 3, T], I32)
        edges = sb("edges", [P, T, 4], I32)
        next_head = sb("next_head", [P, 4], I32)
        lastrow = sb("lastrow", [1, 4], I32)
        dig_i = sb("dig_i", [P, T], I32)
        dig = sb("dig", [P, T])
        onehot = sb("onehot", [P, K, HI], BF16)
        picked = sb("picked", [P, HI])
        rank = sb("rank", [P, K])
        place = sb("place", [P, 2, K], I32)
        moved = sb("moved", [P, 2, K, 4], I32)
        counts = sb("counts", [P, HI])
        totals = sb("totals", [P, HI])
        upto = sb("upto", [P, HI])
        head_f = sb("head_f", [P, T])
        type_f = sb("type_f", [P, T])
        differ = sb("differ", [P, T])
        same = sb("same", [P, T])
        is_end = sb("is_end", [P, T])
        cut = sb("cut", [P, T])
        in_first = sb("in_first", [P, T])
        first_end = sb("first_end", [P, T])
        write_f = sb("write_f", [P, T])
        xs = sb("xs", [P, 2, K, C])
        rowH = sb("rowH", [P, 2, K, W1])
        rowT = sb("rowT", [P, 2, K, W1])
        gi = sb("gi", [P, 2, 3, K], I32)
        rowO = sb("rowO", [P, 2, K, W1])
        typ = sb("typ", [P, K, R])
        sc = sb("sc", [P, K, R])
        e1 = sb("e1", [P, K])
        e2 = sb("e2", [P, K])
        mb = sb("mb", [P, K + 1])
        dl = sb("dl", [P, 2, K])
        ex = sb("ex", [P, 2, K])
        CO_ = sb("decay", [P, CO, K + 1])
        XI = sb("XI", [P, CO, K + 1])
        S = sb("S", [P, CO, K + 1])
        cap = sb("cap", [P, CO, K])
        capm = sb("capm", [P, K])
        part = sb("part", [P, CO + 1])
        first = sb("first", [P, CO + 1])
        v = sb("v", [P, K, C])
        sq = sb("sq", [P, K, C])
        ss = sb("ss", [P, K])
        rs = sb("rs", [P, K])
        mean = sb("mean", [P, K])
        rd = sb("rd", [P, K])
        vT = sb("vT", [C, K * P])
        z = sb("z", [P, K, C])
        dg = sb("dg", [P, P])
        wt = sb("wt", [P, P])
        mm = sb("mm", [P, P])
        sx = sb("sx", [P, P])
        sxT = sb("sxT", [P, P])
        sv = sb("sv", [P, 8])
        seam_i = sb("seam_i", [P, 2], I32)

        psR = pb("psR", [P, 512])
        psM = pb("psM", [P, 512])
        psT = pb("psT", [P, 4, 512])
        psP = pb("psP", [P, 2, 512])
        KT = 4
        KP = K // 2

        s_load = sem("inputs_loaded")
        s_x = [sem(f"x_loaded{b}") for b in range(2)]
        s_xfree = sem("x_chunk_used")
        s_clean = sem("pads_set")
        s_const = sem("constants_made")
        s_dve = sem("vector_chain")
        s_act = sem("scalar_chain")
        s_wp = sem("weights_projected")
        s_tot = sem("sort_totals")
        s_hot = sem("onehot_made")
        s_cnt = sem("counts_added")
        s_read = sem("counts_read")
        s_base = sem("sort_base_ready")
        s_basep = sem("sort_base_in_psum")
        s_plc = sem("places_ready")
        s_sct = [sem(f"edges_scattered{b}") for b in range(2)]
        s_again = sem("edges_reloaded")
        s_idx = sem("indices_ready")
        s_gat = [sem(f"rows_gathered{b}") for b in range(2)]
        s_v = sem("rows_for_projection")
        s_tr = sem("rows_transposed")
        s_trc = sem("transposes_copied")
        s_pr = sem("rows_projected")
        s_node = sem("node_rows_ready")
        s_nst = [sem(f"node_rows_stored{b}") for b in range(2)]
        s_row = sem("edge_rows_ready")
        s_wr = [sem(f"edge_rows_written{b}") for b in range(2)]
        s_dl = sem("exponents_ready")
        s_ex = sem("exponentials_ready")
        s_sq = sem("squares_ready")
        s_rt = sem("roots_ready")
        s_mat = sem("seam_matrix_ready")
        s_bc = sem("seam_matrix_done")
        s_sg = sem("seam_gathered")
        s_sw = sem("seam_written")
        s_si = sem("seam_index_ready")

        s_turn = sem("gpsimd_turns")
        s_turn_pe = sem("tensor_turns")

        block = ctx.enter_context(nc.Block())

        def steps(eng, body, n, peel=1):
            for i in range(peel):
                body(i, True)
            with eng.Fori(peel, n) as i:
                body(i, False)

        DIG = [P, HI]

        def node_stores(b):
            return sum(16 * (4 if j <= rest // K else 3) for j in range(b, NCH, 2))

        def x_loads(j):
            return sum(16 * (2 if i <= rest // K else 1) for i in range(j % 2, j + 1, 2))

        @block.sync
        def _(sp):
            sp.dma_start(w_sb[:, :], fc_w).then_inc(s_load, 16)
            with nc.allow_non_contiguous_dma(reason="a small transposed weight"):
                sp.dma_start(relT[:, :], rel.rearrange("r c -> c r")).then_inc(s_load, 16)
                sp.dma_start(bias_c[:, :], fc_b.rearrange("(c a) -> c a", a=1)).then_inc(s_load, 16)
            sp.wait_ge(s_clean, 1)
            for n, a in enumerate((src, dst, etype)):
                sp.dma_start(raw[0:full, n, :], a[0:full * T].rearrange("(p t) -> p t", t=T)).then_inc(s_load, 16)
                sp.dma_start(raw[full:P, n, 0:rest], a[full * T:N].rearrange("(p t) -> p t", p=1)).then_inc(s_load, 16)
            sp.dma_start(by_head[NPAD:NPAD + 1, :], lastrow[:, :]).then_inc(s_load, 16)

            def x_in(j, static, b, last):
                sp.dma_start(xs[0:full, b, :, :], x[0:full * T, :].rearrange("(p t) c -> p t c", t=T)[:, bass.ds(j * K, K), :]).then_inc(s_x[b], 16)
                if last == "whole":
                    sp.dma_start(xs[full:P, b, :, :], x[full * T:full * T + (rest // K) * K, :].rearrange("(p t) c -> p t c", p=1)[:, bass.ds(j * K, K), :]).then_inc(s_x[b], 16)
                elif last:
                    sp.dma_start(xs[full:P, b, 0:last, :], x[full * T + (rest // K) * K:N, :].rearrange("(p t) c -> p t c", p=1)).then_inc(s_x[b], 16)
            for j in range(2):
                x_in(j, True, j, "whole")

            t0 = table0.rearrange("(p t) w -> p t w", t=T)
            t1 = table1.rearrange("(p t) w -> p t w", t=T)
            o0 = out[0:full * T, :].rearrange("(p t) c -> p t c", t=T)

            def store(j, b, last):
                c = bass.ds(j * K, K)
                sp.wait_ge(s_node, j + 1)
                sp.dma_start(t0[:, c, :], rowT[:, b, :, 0:W0]).then_inc(s_nst[b], 16)
                sp.dma_start(t1[:, c, :], rowH[:, b, :, :]).then_inc(s_nst[b], 16)
                sp.dma_start(o0[:, c, :], rowO[0:full, b, :, 0:C]).then_inc(s_nst[b], 16)
                if last == "whole":
                    sp.dma_start(out[full * T:full * T + (rest // K) * K, :].rearrange("(p t) c -> p t c", p=1)[:, c, :],
                                 rowO[full:P, b, :, 0:C]).then_inc(s_nst[b], 16)
                elif last:
                    sp.dma_start(out[full * T + (rest // K) * K:N, :].rearrange("(p t) c -> p t c", p=1),
                                 rowO[full:P, b, 0:last, 0:C]).then_inc(s_nst[b], 16)

            WH = rest // K
            q = WH // 2

            def whole(i, static):
                for b in range(2):
                    j = i * 2 + b
                    store(j, b, "whole")
                    sp.wait_ge(s_xfree, j + 1)
                    x_in(j + 2, static, b, "whole")
            for i in range(0, q - 1):
                whole(i, True)
            for j in range(2 * (q - 1), NCH):
                b = j % 2
                store(j, b, "whole" if j < WH else (rest % K if j == WH else 0))
                if j + 2 < NCH:
                    sp.wait_ge(s_xfree, j + 1)
                    x_in(j + 2, True, b, "whole" if j + 2 < WH else (rest % K if j + 2 == WH else 0))

            for b in range(2):
                sp.wait_ge(s_sct[b], 16 * K * (NCH // 2))
            sp.dma_start(edges[:, :, :], by_lo.rearrange("(p t) w -> p t w", t=T)).then_inc(s_again, 16)
            for b in range(2):
                sp.wait_ge(s_sct[b], 2 * 16 * K * (NCH // 2))
            sp.dma_start(edges[:, :, :], by_head[0:NPAD, :].rearrange("(p t) w -> p t w", t=T)).then_inc(s_again, 16)
            sp.dma_start(next_head[:, :], by_head[1:NPAD + 1, :].rearrange("(p t) w -> p t w", t=T)[:, T - 1, :]).then_inc(s_again, 16)
            for b in range(2):
                sp.wait_ge(s_nst[b], node_stores(b))
            sp.wait_ge(s_load, 16 * 10)
            sp.wait_ge(s_sw, 32)

        @block.gpsimd
        def _(pool):
            nc.gpsimd.memset(raw[:, 0, :], NPAD - 1).then_inc(s_const, 1)
            nc.gpsimd.memset(raw[:, 1:3, :], 0).then_inc(s_const, 1)
            nc.gpsimd.memset(lastrow[:, :], -1).then_inc(s_const, 1)
            nc.gpsimd.memset(xs[:, :, :, :], 0.0).then_inc(s_const, 1)
            nc.gpsimd.iota(iota_i[:, :], pattern=[[1, HI]], base=0, channel_multiplier=0).then_inc(s_const, 1)
            nc.gpsimd.memset(ones[:, :], 1.0).then_inc(s_const, 1)
            nc.gpsimd.memset(zeros[:, :], 0.0).then_inc(s_const, 1)
            pool.wait_ge(s_const, 7)
            nc.gpsimd.memset(rowT[:, :, :, :], 1.0).then_inc(s_clean, 1)
            nc.gpsimd.affine_select(out=ident[:, :], in_=zeros[:, 0:P], compare_op=ALU.not_equal, fill=1.0,
                                    base=0, pattern=[[-1, P]], channel_multiplier=1).then_inc(s_const, 1)
            nc.gpsimd.affine_select(out=before[:, :], in_=ones[:, :], compare_op=ALU.is_gt, fill=0.0,
                                    base=0, pattern=[[1, P]], channel_multiplier=-1).then_inc(s_const, 1)
            nc.gpsimd.affine_select(out=after[:, :], in_=ones[:, :], compare_op=ALU.is_gt, fill=0.0,
                                    base=0, pattern=[[-1, P]], channel_multiplier=1).then_inc(s_const, 1)
            nc.gpsimd.memset(rowH[:, :, :, :], 1.0).then_inc(s_const, 1)
            nc.gpsimd.memset(rowO[:, :, :, :], 1.0).then_inc(s_const, 1)
            nc.gpsimd.memset(CO_[:, :, :], 0.0).then_inc(s_const, 1)

            for d, to in enumerate((by_lo, by_head[0:NPAD, :])):
                def scatter(i, static, d=d, to=to):
                    for b in range(2):
                        pool.wait_ge(s_plc, d * NCH + i * 2 + b + 1)
                        pool.sem_inc(s_turn, 1)
                        for k in range(K):
                            pool.indirect_dma_start(
                                out=to, out_offset=bass.IndirectOffsetOnAxis(ap=place[:, b, k:k + 1].bitcast(U32), axis=0),
                                in_=moved[:, b, k, :], in_offset=None).then_inc(s_sct[b], 16)
                steps(pool, scatter, NCH // 2)

            for h, (tab, W) in enumerate(((table0, W0), (table1, W1))):
                g = h * NCH
                if h == 0:
                    for b in range(2):
                        pool.wait_ge(s_nst[b], node_stores(b))

                def gather(j, b, tab=tab, W=W, g=g):
                    pool.wait_ge(s_idx, g + j + 1)
                    pool.sem_inc(s_turn, 1)
                    for n, to in ((0, rowH), (1, rowT)):
                        for k in range(K):
                            pool.indirect_dma_start(
                                out=to[:, b, k, 0:W], out_offset=None, in_=tab,
                                in_offset=bass.IndirectOffsetOnAxis(ap=gi[:, b, n, k:k + 1].bitcast(U32), axis=0),
                            ).then_inc(s_gat[b], 16)

                def write(j, b, h=h, g=g):
                    pool.wait_ge(s_row, g + j + 1)
                    pool.sem_inc(s_turn, 1)
                    to, W, top = ((table1, W1, NPAD - 1), (out, C, N - 1))[h]
                    for k in range(K):
                        pool.indirect_dma_start(
                            out=to, out_offset=bass.IndirectOffsetOnAxis(ap=place[:, b, k:k + 1].bitcast(U32), axis=0),
                            in_=rowO[:, b, k, 0:W], in_offset=None, bounds_check=top, oob_is_err=False,
                        ).then_inc(s_wr[b], 16)

                gather(0, 0)

                def pair(i, static):
                    gather(i * 2 + 1, 1)
                    write(i * 2, 0)
                    gather(i * 2 + 2, 0)
                    write(i * 2 + 1, 1)
                steps(pool, pair, NCH // 2 - 1)
                gather(NCH - 1, 1)
                write(NCH - 2, 0)
                write(NCH - 1, 1)
                pool.wait_ge(s_si, 2 * h + 1)
                pool.indirect_dma_start(
                    out=rowH[:, 0, 0, 0:W], out_offset=None, in_=tab,
                    in_offset=bass.IndirectOffsetOnAxis(ap=seam_i[:, 0:1].bitcast(U32), axis=0)).then_inc(s_sg, 16)
                for b in range(2):
                    pool.wait_ge(s_wr[b], (h + 1) * 16 * K * (NCH // 2))
                pool.wait_ge(s_si, 2 * h + 2)
                to, Wo, top = ((table1, W1, NPAD - 1), (out, C, N - 1))[h]
                pool.indirect_dma_start(
                    out=to, out_offset=bass.IndirectOffsetOnAxis(ap=seam_i[:, 1:2].bitcast(U32), axis=0),
                    in_=rowO[:, 0, 0, 0:Wo], in_offset=None, bounds_check=top, oob_is_err=False).then_inc(s_sw, 16)
                pool.wait_ge(s_sw, 16 * (h + 1))

        @block.tensor
        def _(pe):
            pe.wait_ge(s_load, 16 * 10)
            pe.wait_ge(s_const, 13)
            pe.wait_ge(s_wp, 1)
            nc.tensor.matmul(psM[0:C, 0:R], w_sb[:, 0:C], relT[:, :], start=True, stop=True).then_inc(s_bc, 1)
            nc.tensor.matmul(psM[0:C, R:2 * R], w_sb[:, C:2 * C], relT[:, :], start=True, stop=True).then_inc(s_bc, 1)
            nc.tensor.matmul(psM[:, 2 * R:3 * R], bias_rep[:, :], relT[:, :], start=True, stop=True).then_inc(s_bc, 1)
            nproj = [0]

            def project(rows, first, i, K0=K):
                pe.wait_ge(s_v, first + i + 1)
                pe.sem_inc(s_turn_pe, 1)
                for t in range(0, K0, KT):
                    for k in range(t, min(t + KT, K0)):
                        last = nc.tensor.transpose(psT[0:C, t // KT, (k - t) * P:(k - t + 1) * P], rows(k), ident[:, :])
                    last.then_inc(s_tr, 1)
                pe.wait_ge(s_trc, first + i + 1)
                for k in range(K0):
                    last = nc.tensor.matmul(psP[:, k // KP, (k % KP) * 2 * R:(k % KP + 1) * 2 * R],
                                            vT[:, k * P:(k + 1) * P], V[:, :], start=True, stop=True)
                last.then_inc(s_pr, 1)

            for d in range(2):
                D = DIG[d]

                def count(i, static, d=d, D=D):
                    for k in range(K):
                        pe.wait_ge(s_hot, d * T + i * K + k + 1)
                        nc.tensor.matmul(psR[:, 0:D], ident_b[:, :], onehot[:, k, 0:D],
                                         start=static and k == 0, stop=True, skip_group_check=True).then_inc(s_cnt, 1)
                steps(pe, count, NCH)
                pe.wait_ge(s_tot, d + 1)
                nc.tensor.matmul(psR[:, 0:D], before[:, :], counts[:, 0:D], start=True, stop=True)
                nc.tensor.matmul(psM[:, 0:D], ones[:, :], counts[:, 0:D], start=True, stop=True).then_inc(s_base, 1)
                pe.wait_ge(s_basep, d + 1)
                nc.tensor.matmul(psR[:, 0:D], ident[:, :], counts[:, 0:D], start=True, stop=True).then_inc(s_base, 1)

                def add(i, static, d=d, D=D):
                    for k in range(K):
                        pe.wait_ge(s_read, d * T + i * K + k + 1)
                        nc.tensor.matmul(psR[:, 0:D], ident_b[:, :], onehot[:, k, 0:D],
                                         start=False, stop=True, skip_group_check=True).then_inc(s_cnt, 1)
                    if d == 0:
                        if True:
                            pe.wait_ge(s_v, i + 1)
                            pe.sem_inc(s_turn_pe, 1)
                            for t in range(0, K, KT):
                                for k in range(t, min(t + KT, K)):
                                    last = nc.tensor.transpose(psT[0:C, t // KT, (k - t) * P:(k - t + 1) * P], v[:, k, :], ident[:, :])
                                last.then_inc(s_tr, 1)
                            pe.wait_ge(s_trc, i + 1)
                            for k in range(K):
                                last = nc.tensor.matmul(psP[:, k // KP, (k % KP) * 2 * R:(k % KP + 1) * 2 * R],
                                                        vT[:, k * P:(k + 1) * P], V[:, :], start=True, stop=True)
                            last.then_inc(s_pr, 1)
                steps(pe, add, NCH)

            for h in range(2):
                if h == 0:
                    def chunk(i, static):
                        project(lambda k: v[:, k, :], NCH, i)
                    steps(pe, chunk, NCH)
                for n in range(2):
                    pe.wait_ge(s_mat, 4 * h + n + 1)
                    nc.tensor.matmul(psM[:, n * P:(n + 1) * P], ones[:, :], dg[:, :], start=True, stop=True).then_inc(s_bc, 1)
                pe.wait_ge(s_mat, 4 * h + 3)
                nc.tensor.transpose(psM[:, 2 * P:3 * P], sx[:, :], ident[:, :]).then_inc(s_bc, 1)
                pe.wait_ge(s_mat, 4 * h + 4)
                nc.tensor.matmul(psR[:, 0:CO], sxT[:, :], S[:, :, K], start=True, stop=True).then_inc(s_bc, 1)
                if h == 0:
                    project(lambda k: v[:, k, :], 2 * NCH, 0, 1)

        @block.scalar
        def _(act):
            link = Link(act, s_act)
            NTR = -(-K // KT)

            def transposes(done, first, i, K0=K):
                for n in range(-(-K0 // KT)):
                    w = (min((n + 1) * KT, K0) - n * KT) * P
                    act.wait_ge(s_tr, done + i * NTR + n + 1)
                    last = nc.scalar.copy(vT[:, n * KT * P:n * KT * P + w], psT[0:C, n, 0:w])
                    last.then_inc(s_trc if n == -(-K0 // KT) - 1 else s_act, 1)

            def node(i, static):
                act.wait_ge(s_sq, i + 1)
                nc.scalar.activation(rs[:, :], ss[:, :], ACT.Sqrt).then_inc(s_rt, 1)
                transposes(0, 0, i)
            act.wait_ge(s_const, 13)
            def node3(i, static):
                for n in range(3):
                    act.wait_ge(s_sq, 3 * i + n + 1)
                    nc.scalar.activation(rs[:, :], ss[:, :], ACT.Sqrt).then_inc(s_rt, 1)
                    if n == 0:
                        transposes(0, 0, i)
            steps(act, node3, NCH)

            for h in range(2):
                nr = 1 + h
                r0 = (3 * NCH, 4 * NCH + 1)[h]
                e0 = h * (NCH + 2)

                def chunk(i, static, h=h, nr=nr, r0=r0, e0=e0):
                    act.wait_ge(s_dl, e0 + i + 1)
                    nc.scalar.activation(ex[:, :, :], dl[:, :, :], ACT.Exp).then_inc(s_act, 1)
                    link.n += 1
                    act.wait_ge(s_act, link.base + link.n + link.i * link.per)
                    nc.scalar.copy(CO_[:, :, 1:K + 1], ex[:, 0:1, :].to_broadcast([P, CO, K])).then_inc(s_ex, 1)
                    for n in range(nr):
                        act.wait_ge(s_sq, r0 + i * nr + n + 1)
                        nc.scalar.activation(rs[:, :], ss[:, :], ACT.Sqrt).then_inc(s_rt, 1)
                    if h == 0:
                        transposes(NCH * NTR, 0, i)
                        link.n += NTR - 1
                if h == 0:
                    link.base = NCH * (NTR - 1)
                    per = 1 + NTR - 1
                else:
                    per = 1

                def body(i, static, per=per, chunk=chunk):
                    link.enter(i, per)
                    chunk(i, static)
                steps(act, body, NCH)
                link.leave(NCH)
                act.wait_ge(s_dl, e0 + NCH + 1)
                nc.scalar.activation(sx[:, :], mm[:, :], ACT.Exp, bias=sv[:, 2:3]).then_inc(s_mat, 1)
                act.wait_ge(s_dl, e0 + NCH + 2)
                nc.scalar.activation(sv[:, 4:5], sv[:, 3:4], ACT.Exp).then_inc(s_ex, 1)
                for n in range(nr):
                    act.wait_ge(s_sq, r0 + NCH * nr + n + 1)
                    nc.scalar.activation(rs[:, 0:1], ss[:, 0:1], ACT.Sqrt).then_inc(s_rt, 1)
                if h == 0:
                    act.wait_ge(s_tr, 2 * NCH * NTR + 1)
                    nc.scalar.copy(vT[:, 0:P], psT[0:C, 0, 0:P]).then_inc(s_trc, 1)

        @block.vector
        def _(dve):
            ve = nc.vector
            link = Link(dve, s_dve)
            link.plain()

            def wide(a, n=K, c=C):
                return a.unsqueeze(2).to_broadcast([P, n, c])

            dve.wait_ge(s_const, 13)
            dve.wait_ge(s_load, 16 * 10)
            link(ve.tensor_copy(iota_f[:, :], iota_i[:, :]))
            link(ve.tensor_copy(iota_r[:, :], iota_f[:, 0:R]))
            link(ve.tensor_copy(ident_b[:, :], ident[:, :]))
            ve.tensor_copy(bias_rep[:, :], bias_c[:, 0:1].to_broadcast([C, P])).then_inc(s_wp, 1)
            for n in range(3):
                link(ve.tensor_copy(edges[:, :, n], raw[:, n, :]))
            link(ve.memset(edges[:, :, 3], 0))
            dve.wait_ge(s_bc, 3)
            link(ve.tensor_copy(V[:, :], psM[0:C, 0:2 * R]))
            link(ve.tensor_copy(brel[:, :], psM[:, 2 * R:3 * R]))

            def norm(K0, root, inv_src=None):
                dve.wait_ge(s_rt, root)
                link(ve.tensor_scalar(rs[:, 0:K0], rs[:, 0:K0], 1e-12, None, ALU.max))
                link(ve.reciprocal(rs[:, 0:K0], rs[:, 0:K0]))

            def squares(a, K0):
                link(ve.tensor_tensor(sq[:, 0:K0, :], a, a, ALU.mult))
                ve.tensor_reduce(ss[:, 0:K0], sq[:, 0:K0, :], AX.X, ALU.add).then_inc(s_sq, 1)

            def layernorm(K0, root, to):
                link(ve.tensor_reduce(mean[:, 0:K0], z[:, 0:K0, :], AX.X, ALU.add))
                link(ve.tensor_scalar(mean[:, 0:K0], mean[:, 0:K0], 1.0 / C, None, ALU.mult))
                link(ve.tensor_tensor(z[:, 0:K0, :], z[:, 0:K0, :], wide(mean[:, 0:K0], K0), ALU.subtract))
                link(ve.tensor_tensor(sq[:, 0:K0, :], z[:, 0:K0, :], z[:, 0:K0, :], ALU.mult))
                link(ve.tensor_reduce(ss[:, 0:K0], sq[:, 0:K0, :], AX.X, ALU.add))
                ve.tensor_scalar(ss[:, 0:K0], ss[:, 0:K0], 1.0 / C, 1e-5, ALU.mult, ALU.add).then_inc(s_sq, 1)
                dve.wait_ge(s_rt, root)
                link(ve.reciprocal(rs[:, 0:K0], rs[:, 0:K0]))
                link(ve.tensor_tensor(to, z[:, 0:K0, :], wide(rs[:, 0:K0], K0), ALU.mult))

            def node_chunk(j, b, static):
                root = 3 * j
                dve.wait_ge(s_x[b], x_wait(j, b))
                if not (static is True and j < 2):
                    dve.wait_ge(s_nst[b], st_wait(j, b))
                X = xs[:, b, :, :]
                link(ve.tensor_copy(v[:, :, :], X))
                ve.tensor_copy(rowT[:, b, :, 0:C], X).then_inc(s_v, 1)
                squares(X, K)
                link(ve.tensor_copy(rowH[:, b, :, X0:W1], X))
                norm(K, root + 1)
                link(ve.tensor_tensor(rowH[:, b, :, 0:C], X, wide(rs[:, :]), ALU.mult))
                link(ve.tensor_copy(rd[:, :], rs[:, :]))
                dve.wait_ge(s_pr, j + 1)
                for n in range(2):
                    a = psP[:, n, 0:KP * 2 * R].rearrange("p (k r) -> p k r", r=2 * R)
                    kk = slice(n * KP, (n + 1) * KP)
                    link(ve.tensor_copy(rowT[:, b, kk, A0:A0 + 2 * R], a))
                link(ve.tensor_tensor(rowH[:, b, :, A0:A0 + 2 * R], rowT[:, b, :, A0:A0 + 2 * R], wide(rd[:, :], K, 2 * R), ALU.mult))
                br = brel[:, :].unsqueeze(1).to_broadcast([P, K, R])
                link(ve.tensor_tensor(rowT[:, b, :, B0:B0 + R], rowT[:, b, :, B0:B0 + R], br, ALU.add))
                link(ve.tensor_tensor(rowH[:, b, :, B0:B0 + R], rowH[:, b, :, B0:B0 + R], br, ALU.add))
                squares(rowH[:, b, :, 0:C], K)
                norm(K, root + 2)
                link(ve.tensor_tensor(z[:, :, :], rowH[:, b, :, 0:C], wide(rs[:, :]), ALU.mult))
                ve.tensor_tensor(z[:, :, :], z[:, :, :], X, ALU.add).then_inc(s_xfree, 1)
                dve.wait_ge(s_xfree, j + 1)
                layernorm(K, root + 3, rowO[:, b, :, 0:C])
                link_row(s_node, j)

            def link_row(s, j):
                ve.tensor_copy(capm[:, 0:1], rs[:, 0:1]).then_inc(s, 1)

            def x_wait(j, b):
                return x_loads(j)

            def st_wait(j, b):
                return sum(16 * (4 if i <= rest // K else 3) for i in range(b, j, 2))

            scat = [0, 0]
            for d in range(2):
                D = DIG[d]
                if d == 1:
                    dve.wait_ge(s_again, 16)
                if d == 0:
                    link(ve.tensor_scalar(dig_i[:, :], edges[:, :, 0], P - 1, None, ALU.bitwise_and))
                else:
                    link(ve.tensor_scalar(dig_i[:, :], edges[:, :, 0], 7, None, ALU.logical_shift_right))
                link(ve.tensor_copy(dig[:, :], dig_i[:, :]))
                n0 = 2 * d * T

                def count(i, static, d=d, D=D, n0=n0):
                    for k in range(K):
                        if not static:
                            dve.wait_ge(s_cnt, n0 + (i - 1) * K + k + 1)
                        ve.tensor_scalar(onehot[:, k, 0:D], iota_f[:, 0:D], dig[:, bass.ds(i * K + k, 1)], None,
                                         ALU.is_equal).then_inc(s_hot, 1)
                steps(dve, count, NCH)
                dve.wait_ge(s_cnt, n0 + T)
                ve.tensor_copy(counts[:, 0:D], psR[:, 0:D]).then_inc(s_tot, 1)
                dve.wait_ge(s_base, 2 * d + 1)
                link(ve.tensor_copy(totals[:, 0:D], psM[:, 0:D]))
                link(ve.tensor_tensor_scan(upto[:, 0:D], zeros[:, 0:D], totals[:, 0:D], 0.0, ALU.add, ALU.add))
                link(ve.tensor_tensor(upto[:, 0:D], upto[:, 0:D], totals[:, 0:D], ALU.subtract))
                ve.tensor_tensor(counts[:, 0:D], upto[:, 0:D], psR[:, 0:D], ALU.add).then_inc(s_basep, 1)
                dve.wait_ge(s_base, 2 * d + 2)
                n1 = n0 + T

                def ranks(j, b, static, d=d, D=D, n1=n1):
                    for k in range(K):
                        link(ve.tensor_scalar(onehot[:, k, 0:D], iota_f[:, 0:D], dig[:, bass.ds(j * K + k, 1)], None, ALU.is_equal))
                        dve.wait_ge(s_cnt, n1 + j * K + k)
                        ve.tensor_tensor_reduce(out=picked[:, 0:D], in0=onehot[:, k, 0:D], in1=psR[:, 0:D], scale=1.0,
                                                scalar=0.0, op0=ALU.mult, op1=ALU.add,
                                                accum_out=rank[:, k:k + 1]).then_inc(s_read, 1)
                        dve.wait_ge(s_read, d * T + j * K + k + 1)
                    if d == 1 or not (static and j < 2):
                        dve.wait_ge(s_sct[b], 16 * K * (d * (NCH // 2) + half(j, b)))
                    link(ve.tensor_copy(place[:, b, :], rank[:, :]))
                    ve.tensor_copy(moved[:, b, :, :], edges[:, bass.ds(j * K, K), :]).then_inc(s_plc, 1)

                def half(j, b):
                    return (j - b) // 2 if isinstance(j, int) else half_i[0]
                half_i = [None]
                if d == 0:
                    for j in range(NCH):
                        ranks(j, j % 2, True)
                        node_chunk(j, j % 2, True)
                else:
                    def pair(i, static):
                        half_i[0] = i
                        link.enter(i, 2 * (K + 1))
                        for b in range(2):
                            ranks(i * 2 + b, b, static)
                    link.base += link.n
                    steps(dve, pair, NCH // 2)
                    link.leave(NCH // 2)

            dve.wait_ge(s_again, 48)
            link(ve.tensor_copy(head_f[:, :], edges[:, :, 0]))
            link(ve.tensor_copy(type_f[:, :], edges[:, :, 2]))
            link(ve.memset(differ[:, 0:1], 1.0))
            link(ve.tensor_tensor(differ[:, 1:T], head_f[:, 1:T], head_f[:, 0:T - 1], ALU.not_equal))
            link(ve.tensor_copy(is_end[:, 0:T - 1], differ[:, 1:T]))
            link(ve.tensor_copy(sv[:, 0:1], next_head[:, 0:1]))
            link(ve.tensor_tensor(is_end[:, T - 1:T], head_f[:, T - 1:T], sv[:, 0:1], ALU.not_equal))
            link(ve.tensor_scalar(cut[:, :], differ[:, :], -BIG, None, ALU.mult))
            link(ve.tensor_scalar(same[:, :], differ[:, :], -1.0, 1.0, ALU.mult, ALU.add))
            link(ve.memset(same[:, 0:1], 1.0))
            link(ve.tensor_tensor_scan(in_first[:, :], same[:, :], zeros[:, 0:T], 1.0, ALU.mult, ALU.add))
            link(ve.tensor_tensor(first_end[:, :], in_first[:, :], is_end[:, :], ALU.mult))
            link(ve.tensor_scalar(write_f[:, :], is_end[:, :], -FAR, FAR, ALU.mult, ALU.add))
            link(ve.tensor_tensor(write_f[:, :], write_f[:, :], head_f[:, :], ALU.add))
            link(ve.memset(typ[:, :, :], 0.0))

            def indices(j, b):
                cc = bass.ds(j * K, K)
                link(ve.tensor_copy(gi[:, b, 0, :], edges[:, cc, 0]))
                ve.tensor_copy(gi[:, b, 1, :], edges[:, cc, 1]).then_inc(s_idx, 1)

            def finish(h, K0, b, rowsH, root, pr, agg):
                vv = v[:, 0:K0, :]
                link(ve.tensor_tensor(vv, agg, wide(rd[:, 0:K0], K0), ALU.mult))
                link(ve.tensor_tensor(vv, vv, rowsH[:, :, 0:C], ALU.add))
                squares(vv, K0)
                norm(K0, root + 1)
                link(ve.tensor_tensor(vv, vv, wide(rs[:, 0:K0], K0), ALU.mult))
                if h == 0:
                    ve.tensor_copy(rowO[:, b, 0:K0, 0:C], vv).then_inc(s_v, 1)
                    link(ve.tensor_copy(rowO[:, b, 0:K0, X0:W1], rowsH[:, :, 0:C]))
                    dve.wait_ge(s_pr, pr)
                    for n in range(2 if K0 > 1 else 1):
                        kk = slice(n * KP, min((n + 1) * KP, K0))
                        w = kk.stop - kk.start
                        a = psP[:, n, 0:w * 2 * R].rearrange("p (k r) -> p k r", r=2 * R)
                        link(ve.tensor_copy(rowO[:, b, kk, A0:A0 + 2 * R], a))
                    br = brel[:, :].unsqueeze(1).to_broadcast([P, K0, R])
                    link(ve.tensor_tensor(rowO[:, b, 0:K0, B0:B0 + R], rowO[:, b, 0:K0, B0:B0 + R], br, ALU.add))
                else:
                    link(ve.tensor_tensor(z[:, 0:K0, :], vv, rowsH[:, :, X0:W1], ALU.add))
                    layernorm(K0, root + 2, rowO[:, b, 0:K0, 0:C])

            PER = (29, 33)
            for h in range(2):
                nr, r0, e0, x0 = 1 + h, (3 * NCH, 4 * NCH + 1)[h], h * (NCH + 2), h * (NCH + 1)
                link(ve.memset(mb[:, :], -BIG))
                link(ve.memset(S[:, :, :], 0.0))
                link(ve.memset(first[:, :], 0.0))
                indices(0, 0)

                def chunk(j, b, static, ahead, i, h=h, nr=nr, r0=r0, e0=e0, x0=x0):
                    if ahead:
                        indices(j + 1, 1 - b)
                    cc = bass.ds(j * K, K)
                    H, Tl = rowH[:, b, :, :], rowT[:, b, :, :]
                    link(ve.tensor_tensor(typ[:, :, :], iota_r[:, :].unsqueeze(1).to_broadcast([P, K, R]),
                                          wide(type_f[:, cc], K, R), ALU.is_equal))
                    dve.wait_ge(s_gat[b], 16 * 2 * K * (h * (NCH // 2) + i + 1))
                    link(ve.tensor_tensor(sc[:, :, :], H[:, :, A0:A0 + R], Tl[:, :, B0:B0 + R], ALU.add))
                    link(ve.tensor_tensor(sc[:, :, :], sc[:, :, :], typ[:, :, :], ALU.mult))
                    link(ve.tensor_reduce(e1[:, :], sc[:, :, :], AX.X, ALU.add))
                    link(ve.scalar_tensor_tensor(e2[:, :], e1[:, :], 0.2, e1[:, :], ALU.mult, ALU.max))
                    link(ve.tensor_copy(mb[:, 0:1], mb[:, K:K + 1]))
                    link(ve.tensor_tensor_scan(mb[:, 1:K + 1], cut[:, cc], e2[:, :], mb[:, 0:1], ALU.add, ALU.max))
                    link(ve.tensor_tensor(dl[:, 0, :], mb[:, 0:K], mb[:, 1:K + 1], ALU.subtract))
                    link(ve.tensor_tensor(dl[:, 0, :], dl[:, 0, :], cut[:, cc], ALU.add))
                    ve.tensor_tensor(dl[:, 1, :], e2[:, :], mb[:, 1:K + 1], ALU.subtract).then_inc(s_dl, 1)
                    link(ve.tensor_copy(XI[:, :, 0], S[:, :, K]))
                    dve.wait_ge(s_ex, x0 + j + 1)
                    link(ve.tensor_tensor(XI[:, :, 1:K + 1], Tl[:, :, 0:CO].rearrange("p k c -> p c k"),
                                          ex[:, 1:2, :].to_broadcast([P, CO, K]), ALU.mult))
                    link(ve.tensor_tensor_scan(S[:, :, :].rearrange("p c k -> p (c k)"), CO_[:, :, :].rearrange("p c k -> p (c k)"),
                                               XI[:, :, :].rearrange("p c k -> p (c k)"), 0.0, ALU.mult, ALU.add))
                    fe = first_end[:, cc]
                    link(ve.tensor_tensor(cap[:, :, :], S[:, :, 1:K + 1], fe.unsqueeze(1).to_broadcast([P, CO, K]), ALU.mult))
                    link(ve.tensor_reduce(part[:, 0:CO], cap[:, :, :], AX.X, ALU.add))
                    link(ve.tensor_tensor(capm[:, :], mb[:, 1:K + 1], fe, ALU.mult))
                    link(ve.tensor_reduce(part[:, CO:CO + 1], capm[:, :], AX.X, ALU.add))
                    link(ve.tensor_tensor(first[:, :], first[:, :], part[:, :], ALU.add))
                    link(ve.reciprocal(rd[:, :], S[:, C, 1:K + 1]))
                    if h == 1 or not static:
                        dve.wait_ge(s_wr[b], 16 * K * (h * (NCH // 2) + i))
                    finish(h, K, b, H, r0 + j * nr, NCH + j + 1, S[:, 0:C, 1:K + 1].rearrange("p c k -> p k c"))
                    ve.tensor_copy(place[:, b, :], write_f[:, cc]).then_inc(s_row, 1)

                def pair(i, static, h=h):
                    link.enter(i, 2 * PER[h])
                    chunk(i * 2, 0, static, True, i)
                    chunk(i * 2 + 1, 1, static, True, i)
                link.base += link.n
                steps(dve, pair, NCH // 2 - 1)
                link.leave(NCH // 2 - 1)
                i = NCH // 2 - 1
                chunk(NCH - 2, 0, False, True, i)
                chunk(NCH - 1, 1, False, False, i)

                fh, lh, mF, mL = head_f[:, 0:1], head_f[:, T - 1:T], first[:, CO:CO + 1], mb[:, K:K + 1]
                link(ve.tensor_copy(seam_i[:, 0:1], fh))
                link(ve.tensor_reduce(sv[:, 1:2], first_end[:, :], AX.X, ALU.max))
                link(ve.tensor_scalar(sv[:, 0:1], sv[:, 1:2], -FAR, FAR, ALU.mult, ALU.add))
                link(ve.tensor_tensor(sv[:, 0:1], sv[:, 0:1], fh, ALU.add))
                ve.tensor_copy(seam_i[:, 1:2], sv[:, 0:1]).then_inc(s_si, 1)
                bc0 = 3 + 4 * h
                for n, a in enumerate((lh, mL)):
                    ve.tensor_scalar(dg[:, :], ident[:, :], a, None, ALU.mult).then_inc(s_mat, 1)
                    dve.wait_ge(s_bc, bc0 + n + 1)
                link(ve.tensor_scalar(wt[:, :], psM[:, 0:P], fh, None, ALU.is_equal))
                link(ve.tensor_tensor(wt[:, :], wt[:, :], after[:, :], ALU.mult))
                link(ve.tensor_tensor(mm[:, :], wt[:, :], psM[:, P:2 * P], ALU.mult))
                link(ve.tensor_scalar(wt[:, :], wt[:, :], BIG, -BIG, ALU.mult, ALU.add))
                link(ve.tensor_tensor(mm[:, :], mm[:, :], wt[:, :], ALU.add))
                link(ve.tensor_reduce(sv[:, 2:3], mm[:, :], AX.X, ALU.max))
                link(ve.tensor_tensor(sv[:, 2:3], sv[:, 2:3], mF, ALU.max))
                link(ve.tensor_tensor(sv[:, 3:4], mF, sv[:, 2:3], ALU.subtract))
                ve.tensor_scalar(sv[:, 2:3], sv[:, 2:3], -1.0, None, ALU.mult).then_inc(s_dl, 1)
                dve.wait_ge(s_bc, bc0 + 3)
                link(ve.tensor_copy(dg[:, :], psM[:, 2 * P:3 * P]))
                ve.tensor_copy(sxT[:, :], dg[:, :]).then_inc(s_mat, 1)
                ve.tensor_copy(capm[:, 0:1], sv[:, 3:4]).then_inc(s_dl, 1)
                dve.wait_ge(s_ex, x0 + NCH + 1)
                link(ve.tensor_scalar(first[:, 0:CO], first[:, 0:CO], sv[:, 4:5], None, ALU.mult))
                dve.wait_ge(s_bc, bc0 + 4)
                link(ve.tensor_tensor(first[:, 0:CO], first[:, 0:CO], psR[:, 0:CO], ALU.add))
                link(ve.tensor_scalar(first[:, C:CO], first[:, C:CO], 1e-30, None, ALU.max))
                link(ve.reciprocal(rd[:, 0:1], first[:, C:CO]))
                dve.wait_ge(s_sg, 16 * (h + 1))
                dve.wait_ge(s_wr[0], (h + 1) * 16 * K * (NCH // 2))
                finish(h, 1, 0, rowH[:, 0, 0:1, :], r0 + NCH * nr, 2 * NCH + 1, first[:, 0:C].unsqueeze(1))
                ve.tensor_copy(capm[:, 0:1], rs[:, 0:1]).then_inc(s_si, 1)


_INS = ['x', 'src', 'dst', 'edge_type_20', 'L0_gnn_relation_emb', 'L0_gnn_fc_w', 'L0_gnn_fc_b']


def kernel(**inputs):
    import numpy as _np
    import concourse.bacc as _bacc
    from concourse import mybir as _mybir
    from concourse.bass_utils import run_bass_kernel_spmd as _run

    nc = _bacc.Bacc("TRN2", target_bir_lowering=False, num_devices=1)
    arrays, args = {}, []
    for name in _INS:
        a = _np.ascontiguousarray(inputs[name])
        arrays[f"in_{name}"] = a
        args.append(nc.dram_tensor(f"in_{name}", a.shape, _mybir.dt.from_np(a.dtype), kind="ExternalInput").ap())
    out = nc.dram_tensor("out_0", inputs['x'].shape, _mybir.dt.float32, kind="ExternalOutput").ap()
    build_gnn(nc, *args, out)
    r = _run(nc, [arrays], core_ids=[0])
    return r.results[0]["out_0"]
```

```python
from contextlib import ExitStack

import concourse.bass as bass
from concourse import mybir

F32, F16, I32, U32 = mybir.dt.float32, mybir.dt.float16, mybir.dt.int32, mybir.dt.uint32
ALU = mybir.AluOpType
ACT = mybir.ActivationFunctionType
AX = mybir.AxisListType

P = 128
BIG = 1.0e30
FAR = 4.0e6


class Link:

    def __init__(self, eng, sem):
        self.eng, self.sem, self.base = eng, sem, 0
        self.plain()

    def enter(self, i, per):
        self.i, self.per, self.n = i, per, 0

    def plain(self):
        self.i, self.per, self.n = 0, 0, 0

    def leave(self, steps):
        assert self.per == 0 or self.n == self.per, (self.n, self.per)
        self.base += steps * self.n
        self.plain()

    def __call__(self, ins, meanwhile=None):
        ins.then_inc(self.sem, 1)
        self.n += 1
        if meanwhile:
            meanwhile()
        self.eng.wait_ge(self.sem, self.base + self.n + self.i * self.per)


def build_gnn(nc, x, src, dst, etype, rel, fc_w, fc_b, out):
    N, C = x.shape
    E = src.shape[0]
    R = rel.shape[0]
    K = 14
    T = 2 * K * -(-max(N, E) // (P * 2 * K))
    NCH = T // K
    G = K // 2
    NPAD = P * T
    HI = NPAD // P
    CO = C + 1
    B0 = CO
    A0, X0, W1 = CO + R, CO + 2 * R, 2 * C + 1 + 2 * R
    WT, WH = CO + R, C + R
    full, rest = (E // T, E % T)
    PN, KN = 125, 16
    TN = N // PN
    NCN = TN // KN
    PS = 120
    assert E == N and HI <= 512 and full == P - 1 and PN * NCN * KN == N and NCN % 2 and NCN < NCH

    def dram(name, shape, dt=F32):
        return nc.dram_tensor(name, shape, dt, kind="Internal").ap()

    tail0 = dram("tail0", [N, WT])
    head0 = dram("head0", [NPAD, WH])
    tail1 = dram("tail1", [NPAD + N, WT])
    rows1 = dram("rows1", [NPAD, W1])
    by_lo = dram("by_lo", [NPAD, 4], I32)
    by_head = dram("by_head", [NPAD + 1, 4], I32)

    ctx = ExitStack()
    with ctx:
        def sb(name, shape, dt=F32):
            return ctx.enter_context(nc.sbuf_tensor(name, shape, dt))

        def pb(name, shape, dt=F32):
            return ctx.enter_context(nc.psum_tensor(name, shape, dt))

        def sem(name):
            return ctx.enter_context(nc.semaphore(name))

        iota_i = sb("iota_i", [P, HI], I32)
        node_i = sb("node_i", [P, HI], I32)
        node_f = sb("node_f", [P, HI])
        spot_i = sb("spot_i", [P, 1], I32)
        spot_f = sb("spot_f", [P, 1])
        iota_h = sb("iota_h", [P, HI], F16)
        iota_r = sb("iota_r", [P, R])
        ident = sb("ident", [P, P])
        ident_h = sb("ident_h", [P, P], F16)
        ones = sb("ones", [P, P])
        before = sb("before", [P, P])
        upto_p = sb("upto_p", [P, P])
        after = sb("after", [P, P])
        zeros = sb("zeros", [P, HI])
        w_sb = sb("w_sb", [C, 2 * C])
        relT = sb("relT", [C, R])
        bias_c = sb("bias_c", [C, 1])
        bias_rep = sb("bias_rep", [C, P])
        V = sb("V", [CO, 3 * R])
        eps = sb("eps", [P, 1])
        brel = sb("brel", [P, R])
        raw = sb("raw", [P, 3, T], I32)
        edges = sb("edges", [P, T, 4], I32)
        next_head = sb("next_head", [P, 4], I32)
        lastrow = sb("lastrow", [1, 4], I32)
        dig_i = sb("dig_i", [P, T], I32)
        dig = sb("dig", [P, T])
        dig2 = sb("dig2", [P, T])
        onehot = sb("onehot", [P, K, HI], F16)
        onehot2 = sb("onehot2", [P, K, P], F16)
        picked = sb("picked", [P, 4, HI])
        tri = sb("tri", [P, G, G])
        prior = sb("prior", [P, T])
        rank = sb("rank", [P, K])
        place = sb("place", [P, 2, K], I32)
        moved = sb("moved", [P, 2, K, 4], I32)
        counts = sb("counts", [P, HI])
        totals = sb("totals", [P, HI])
        starts = sb("starts", [P, HI])
        row_i = sb("row_i", [P, HI], I32)
        part_i = sb("part_i", [P, HI], I32)
        row_of = sb("row_of", [P, HI])
        lot = sb("lot", [P, K, P], F16)
        lotT = sb("lotT", [P, K * P], F16)
        row_p = sb("row_p", [P, 2, HI], F16)
        tail_row = sb("tail_row", [P, T], I32)
        head_f = sb("head_f", [P, T])
        type_f = sb("type_f", [P, T])
        differ = sb("differ", [P, T])
        in_last = differ
        is_end = sb("is_end", [P, T])
        not_end = sb("not_end", [P, T])
        mid_end = sb("mid_end", [P, T])
        cut = sb("cut", [P, T])
        in_first = sb("in_first", [P, T])
        first_end = sb("first_end", [P, T])
        write_f = sb("write_f", [P, T])
        AE = sb("AE", [P, R, T])
        half_less = write_f
        signs = picked[:, :, :].rearrange("p k d -> p (k d)")[:, 0:HI + 1]
        AE_all = AE[:, :, :].rearrange("p r t -> p (r t)")
        same = AE_all[:, 0:T * G].rearrange("p (n a b) -> p n a b", a=G, b=G)
        rows_of = (onehot, AE_all[:, 0:K * HI // 2].bitcast(F16).rearrange("p (k d) -> p k d", d=HI))
        picks = AE_all[:, T * G:T * G + G * HI].rearrange("p (k d) -> p k d", d=HI)
        area = sb("area", [P, KN * (5 * C + 2 * C + 4 * WT + 2 * WH + R)])
        taken = [0]

        def carve(*dims):
            n = 1
            for d in dims:
                n *= d
            a = area[:, taken[0]:taken[0] + n]
            taken[0] += n
            names = "abc"[:len(dims)]
            return a.rearrange(f"p ({' '.join(names)}) -> p {' '.join(names)}", **dict(zip(names[1:], dims[1:])))
        xs = carve(2, KN, C)
        xc = carve(KN, C)
        nT = carve(2, KN, WT)
        nH = carve(2, KN, WH)
        n1 = carve(2, KN, WT)
        nout = carve(2, KN, C)
        nsq = carve(KN, C)
        nB = carve(2, KN // 2, R)
        ns = sb("ns", [P, 12, KN])
        taken[0] = 0
        rowH = carve(2, K, W1)
        rowT = carve(2, K, WT)
        rowO = carve(2, K, W1)
        v = carve(K, C)
        sq = carve(K, C)
        gi = sb("gi", [P, 2, 2, K], I32)
        typ = sb("typ", [P, K, R])
        sc = sb("sc", [P, K, R])
        e1 = sb("e1", [P, K])
        e2 = sb("e2", [P, K])
        dl = sb("dl", [P, 2, K])
        ex = sb("ex", [P, 2, K])
        decay = sb("decay", [P, CO, K + 1])
        XI = sb("XI", [P, CO, K + 1])
        SM = sb("SM", [P, CO + 1, K + 1])
        S, mb = SM[:, 0:CO, :], SM[:, CO, :]
        cap = sb("cap", [P, CO + 1, K])
        capm = sb("capm", [P, K])
        part = sb("part", [P, CO + 1])
        first = sb("first", [P, CO + 1])
        ss = sb("ss", [P, K])
        rs = sb("rs", [P, K])
        mean = sb("mean", [P, K])
        rd = sb("rd", [P, K])
        vT = sb("vT", [CO, KN * P])
        dg = sb("dg", [P, 2, P])
        wt = sb("wt", [P, P])
        mm = sb("mm", [P, P])
        sx = sb("sx", [P, P])
        sxT = sb("sxT", [P, P])
        sv = sb("sv", [P, 12])
        seam_i = sb("seam_i", [P, 5], I32)
        seam_row = counts[:, 0:W1]
        first_A = counts[:, W1:W1 + R]
        last_row = totals[:, 0:W1]
        earlier = starts[:, 0:P]
        not_earlier = starts[:, P:2 * P]

        KT = 4
        psR = [pb(f"psR{b}", [P, 512]) for b in range(2)]
        psT = pb("psT", [P, 4, 512])
        psP = pb("psP", [P, 2, 512])
        psM = psT[:, 3, :]
        psL = (psR[0], psR[1], psP[:, 0, :], psP[:, 1, :])

        s_src = sem("heads_loaded")
        s_load = sem("inputs_loaded")
        s_set = sem("more_constants_made")
        s_x = [sem(f"x_loaded{b}") for b in range(2)]
        s_clean = sem("pads_set")
        s_const = sem("constants_made")
        s_dve = sem("vector_chain")
        s_act = sem("scalar_chain")
        s_mat = sem("small_matrix_ready")
        s_bc = sem("small_matrix_done")
        s_turn = sem("gpsimd_turns")
        s_turn_pe = sem("tensor_turns")
        s_half = sem("digits_for_signs_ready")
        s_one = sem("count_onehots_made")
        s_oned = sem("count_onehots_added")
        s_sgn = sem("count_signs_made")
        s_sgnd = sem("count_signs_added")
        s_hot = sem("onehot_made")
        s_cnt = sem("counts_added")
        s_tot = sem("partition_counts_copied")
        s_read = sem("counts_read")
        s_base = sem("sort_base_multiplied")
        s_basep = sem("sort_base_ready")
        s_plc = sem("places_ready")
        s_sct = [sem(f"edges_scattered{b}") for b in range(2)]
        s_again = sem("edges_reloaded")
        s_map = sem("head_counts_copied")
        s_mapd = sem("head_counts_summed")
        s_cen = sem("node_rows_centred")
        s_nsq = sem("node_squares_made")
        s_nroot = sem("node_root_asked")
        s_nrt = sem("node_root_made")
        s_ntr = sem("node_transposed")
        s_ntc = sem("node_transposes_copied")
        s_npr = sem("node_projected")
        s_nb = sem("node_projections_copied")
        s_nr = sem("node_scale_ready")
        s_nact = sem("node_rows_scaled")
        s_node = sem("node_rows_ready")
        s_nst = [sem(f"node_rows_stored{b}") for b in range(2)]
        s_idx = sem("chunk_buffers_free")
        s_gat = [sem(f"rows_gathered{b}") for b in range(2)]
        s_hl = [sem(f"head_rows_loaded{b}") for b in range(2)]
        s_v = sem("rows_for_projection")
        s_tr = sem("rows_transposed")
        s_trc = sem("transposes_copied")
        s_pr = sem("rows_projected")
        s_xc = sem("head_x_copied")
        s_out = sem("projections_copied")
        s_kept = sem("projections_kept")
        s_spread = sem("head_projections_spread")
        s_row = sem("edge_rows_ready")
        s_dump = [sem(f"edge_rows_stored{b}") for b in range(2)]
        s_wr = [sem(f"node_rows_written{b}") for b in range(2)]
        s_dl = sem("exponents_ready")
        s_ex = sem("exponentials_ready")
        s_sq = sem("rows_to_square")
        s_sqd = sem("rows_squared")
        s_ask = sem("roots_asked")
        s_rt = sem("roots_ready")
        s_lo = sem("tail_lows_ready")
        s_lt = sem("tail_lows_transposed")
        s_ltc = sem("tail_lows_copied")
        s_look = sem("tails_looked_up")
        s_took = sem("tail_rows_taken")
        s_sg = sem("seam_gathered")
        s_lr = sem("last_rows_gathered")
        s_si = sem("seam_index_ready")
        s_sw = sem("seam_written")

        block = ctx.enter_context(nc.Block())
        NP2, NN2 = NCH // 2, NCN // 2

        def steps(eng, body, n, at=0):
            body(at, True)
            with eng.Fori(at + 1, n) as i:
                body(i, False)

        def cols(j, n=K):
            return bass.ds(j * n, n)

        node_halves = ((0, PS), (PS, PN))
        LAG = 2
        assert NCN + LAG <= NCH
        Q = 4
        assert NCH % Q == 0

        def count_parts(d):
            nv = (9, 10)[d]
            v0, a0 = -(-nv // 2), nv + -(-(K - nv) // 2)
            return (range(0, v0), range(v0, nv)), (range(nv, a0), range(a0, K)), nv, K - nv
        NST = 4 * 2 * 16

        @block.sync
        def _(sp):
            sp.wait_ge(s_clean, 1)
            for n, a in enumerate((src, dst, etype)):
                sp.dma_start(raw[0:full, n, :], a[0:full * T].rearrange("(p t) -> p t", t=T)).then_inc(s_load if n else s_src, 16)
                sp.dma_start(raw[full:P, n, 0:rest], a[full * T:E].rearrange("(p t) -> p t", p=1)).then_inc(s_load if n else s_src, 16)
            sp.dma_start(w_sb[:, :], fc_w).then_inc(s_load, 16)
            with nc.allow_non_contiguous_dma(reason="a small transposed weight"):
                sp.dma_start(relT[:, :], rel.rearrange("r c -> c r")).then_inc(s_load, 16)
                sp.dma_start(bias_c[:, :], fc_b.rearrange("(c a) -> c a", a=1)).then_inc(s_load, 16)
            sp.dma_start(by_head[NPAD:NPAD + 1, :], lastrow[:, :]).then_inc(s_load, 16)
            sp.dma_start(head0[N:N + P, :], zeros[:, 0:WH]).then_inc(s_load, 16)
            sp.dma_start(head0[N + P:NPAD, :], zeros[0:NPAD - N - P, 0:WH]).then_inc(s_load, 16)

            xv = x.rearrange("(p t) c -> p t c", t=TN)
            t0 = tail0.rearrange("(p t) w -> p t w", t=TN)
            h0 = head0[0:N, :].rearrange("(p t) w -> p t w", t=TN)
            t1 = tail1[NPAD:NPAD + N, :].rearrange("(p t) w -> p t w", t=TN)
            ov = out.rearrange("(p t) c -> p t c", t=TN)

            def x_in(j, b):
                for lo, hi in node_halves:
                    sp.dma_start(xs[lo:hi, b, :, :], xv[lo:hi, cols(j, KN), :]).then_inc(s_x[b], 16)

            def store(j, b):
                sp.wait_ge(s_node, j + 1)
                sp.wait_ge(s_nact, j + 1)
                for to, of in ((t0, nT), (h0, nH), (t1, n1), (ov, nout)):
                    for lo, hi in node_halves:
                        sp.dma_start(to[lo:hi, cols(j, KN), :], of[lo:hi, b, :, :]).then_inc(s_nst[b], 16)

            x_in(0, 0)
            x_in(1, 1)

            def nodes(i, static):
                store(i * 2, 0)
                x_in(i * 2 + 2, 0)
                store(i * 2 + 1, 1)
                x_in(i * 2 + 3, 1)
            steps(sp, nodes, NN2 - 1)
            store(NCN - 3, 0)
            x_in(NCN - 1, 0)
            store(NCN - 2, 1)
            store(NCN - 1, 0)

            for b in range(2):
                sp.wait_ge(s_sct[b], 16 * K * NP2)
            sp.dma_start(edges[:, :, :], by_lo.rearrange("(p t) w -> p t w", t=T)).then_inc(s_again, 16)
            for b in range(2):
                sp.wait_ge(s_sct[b], 2 * 16 * K * NP2)
            sp.dma_start(edges[:, :, :], by_head[0:NPAD, :].rearrange("(p t) w -> p t w", t=T)).then_inc(s_again, 16)
            sp.dma_start(next_head[:, :], by_head[1:NPAD + 1, :].rearrange("(p t) w -> p t w", t=T)[:, T - 1, :]).then_inc(s_again, 16)

            te = tail1[0:NPAD, :].rearrange("(p t) w -> p t w", t=T)
            re = rows1.rearrange("(p t) w -> p t w", t=T)

            def dump(i, static):
                for b in range(2):
                    j = i * 2 + b
                    sp.wait_ge(s_out, j + 1)
                    sp.dma_start(re[:, cols(j), :], rowO[:, b, :, :]).then_inc(s_dump[b], 16)
                    sp.dma_start(te[:, cols(j), :], rowO[:, b, :, 0:WT]).then_inc(s_dump[b], 16)
            steps(sp, dump, NP2)

            sp.wait_ge(s_sw, 32)

            def heads(i, static):
                for b in range(2):
                    j = i * 2 + b
                    sp.wait_ge(s_idx, NCH + j + 1)
                    sp.dma_start(rowH[:, b, :, :], re[:, cols(j), :]).then_inc(s_hl[b], 16)
            steps(sp, heads, NP2)

            for b in range(2):
                sp.wait_ge(s_nst[b], NST * (NN2 + 1 - b))
                sp.wait_ge(s_dump[b], 32 * NP2)
            sp.wait_ge(s_load, 16 * 10)
            sp.wait_ge(s_sw, 48)

        @block.gpsimd
        def _(pool):
            gp = nc.gpsimd
            gp.memset(raw[:, 0, :], NPAD - 1).then_inc(s_const, 1)
            gp.memset(raw[:, 1:3, :], 0).then_inc(s_const, 1)
            gp.memset(lastrow[:, :], -1).then_inc(s_const, 1)
            gp.memset(zeros[:, :], 0.0).then_inc(s_const, 1)
            pool.wait_ge(s_const, 4)
            gp.iota(iota_i[:, :], pattern=[[1, HI]], base=0, channel_multiplier=0).then_inc(s_clean, 1)
            gp.memset(ones[:, :], 1.0).then_inc(s_const, 1)
            gp.iota(node_i[:, :], pattern=[[P, HI]], base=NPAD, channel_multiplier=1).then_inc(s_const, 1)
            gp.iota(spot_i[:, :], pattern=[[0, 1]], base=-1, channel_multiplier=T).then_inc(s_const, 1)
            pool.wait_ge(s_const, 7)
            gp.affine_select(out=ident[:, :], in_=zeros[:, 0:P], compare_op=ALU.not_equal, fill=1.0,
                             base=0, pattern=[[-1, P]], channel_multiplier=1).then_inc(s_const, 1)
            gp.affine_select(out=before[:, :], in_=ones[:, :], compare_op=ALU.is_gt, fill=0.0,
                             base=0, pattern=[[1, P]], channel_multiplier=-1).then_inc(s_const, 1)
            gp.affine_select(out=upto_p[:, :], in_=ones[:, :], compare_op=ALU.is_ge, fill=0.0,
                             base=0, pattern=[[1, P]], channel_multiplier=-1).then_inc(s_const, 1)
            gp.affine_select(out=after[:, :], in_=ones[:, :], compare_op=ALU.is_gt, fill=0.0,
                             base=0, pattern=[[-1, P]], channel_multiplier=1).then_inc(s_const, 1)
            for a in (nT, n1):
                gp.memset(a[:, :, :, C:CO], 1.0).then_inc(s_const, 1)
            gp.memset(decay[:, :, :], 0.0).then_inc(s_const, 1)
            gp.affine_select(out=tri[:, :, :], in_=ones[:, 0:G * G].rearrange("p (a b) -> p a b", b=G),
                             compare_op=ALU.is_gt, fill=0.0, base=0, pattern=[[1, G], [-1, G]],
                             channel_multiplier=0).then_inc(s_const, 1)

            pool.wait_ge(s_const, 15)
            pool.wait_ge(s_clean, 1)
            for of, to in ((iota_i[:, 0:R], iota_r), (node_i, node_f), (spot_i, spot_f)):
                gp.tensor_copy(to[:, :], of[:, :]).then_inc(s_set, 1)
            gp.memset(eps[:, :], 1e-5).then_inc(s_set, 1)
            pool.wait_ge(s_set, 4)
            gp.memset(vT[C:CO, :], 1.0).then_inc(s_set, 1)
            pool.wait_ge(s_set, 5)
            gp.memset(V[C:CO, :], 0.0).then_inc(s_set, 1)
            pool.wait_ge(s_set, 6)
            pool.wait_ge(s_src, 32)
            pool.wait_ge(s_load, 16 * 10)
            for n in range(3):
                gp.tensor_copy(edges[:, :, n], raw[:, n, :]).then_inc(s_set, 1)
            gp.memset(edges[:, :, 3], 0).then_inc(s_set, 1)
            gp.tensor_copy(bias_rep[:, :], bias_c[:, 0:1].to_broadcast([C, P])).then_inc(s_set, 1)

            for d, to in enumerate((by_lo, by_head[0:NPAD, :])):
                def scatter(i, static, d=d, to=to):
                    for b in range(2):
                        pool.wait_ge(s_plc, d * NCH + i * 2 + b + 1)
                        pool.sem_inc(s_turn, 1)
                        for k in range(K):
                            pool.indirect_dma_start(
                                out=to, out_offset=bass.IndirectOffsetOnAxis(ap=place[:, b, k:k + 1].bitcast(U32), axis=0),
                                in_=moved[:, b, k, :], in_offset=None).then_inc(s_sct[b], 16)
                steps(pool, scatter, NP2)

            def gather(j, b, n, tab, to):
                for k in range(K):
                    pool.indirect_dma_start(
                        out=to[:, b, k, 0:tab.shape[1]], out_offset=None, in_=tab,
                        in_offset=bass.IndirectOffsetOnAxis(ap=gi[:, b, n, k:k + 1].bitcast(U32), axis=0),
                    ).then_inc(s_gat[b], 16)

            for b in range(2):
                pool.wait_ge(s_nst[b], NST * (NN2 + 1 - b))
            pool.wait_ge(s_load, 16 * 10)
            gp.memset(rowO[:, :, :, C:CO], 1.0).then_inc(s_const, 1)
            pool.wait_ge(s_const, 16)

            def both(i, static):
                for b in range(2):
                    pool.wait_ge(s_idx, i * 2 + b + 1)
                    pool.sem_inc(s_turn, 1)
                    gather(i * 2 + b, b, 0, head0, rowH)
                    gather(i * 2 + b, b, 1, tail0, rowT)
            steps(pool, both, NP2)

            pool.wait_ge(s_si, 1)
            pool.indirect_dma_start(
                out=seam_row[:, 0:WH], out_offset=None, in_=head0,
                in_offset=bass.IndirectOffsetOnAxis(ap=seam_i[:, 0:1].bitcast(U32), axis=0)).then_inc(s_sg, 16)
            for b in range(2):
                pool.wait_ge(s_dump[b], 32 * NP2)
            pool.wait_ge(s_si, 2)
            for to, w in ((tail1[0:NPAD, :], WT), (rows1, W1)):
                pool.indirect_dma_start(
                    out=to, out_offset=bass.IndirectOffsetOnAxis(ap=seam_i[:, 1:2].bitcast(U32), axis=0),
                    in_=rowO[:, 0, 0, 0:w], in_offset=None, bounds_check=NPAD - 1, oob_is_err=False).then_inc(s_sw, 16)
            pool.wait_ge(s_sw, 32)
            for n, to, done in ((2, last_row, s_lr), (3, seam_row, s_sg)):
                pool.indirect_dma_start(
                    out=to, out_offset=None, in_=rows1,
                    in_offset=bass.IndirectOffsetOnAxis(ap=seam_i[:, n:n + 1].bitcast(U32), axis=0)).then_inc(done, 16)

            def tails(j, b):
                pool.wait_ge(s_idx, NCH + j + 1)
                pool.sem_inc(s_turn, 1)
                gather(j, b, 1, tail1, rowT)

            def write(j, b):
                pool.wait_ge(s_row, j + 1)
                pool.sem_inc(s_turn, 1)
                for k in range(K):
                    pool.indirect_dma_start(
                        out=out, out_offset=bass.IndirectOffsetOnAxis(ap=place[:, b, k:k + 1].bitcast(U32), axis=0),
                        in_=rowO[:, b, k, 0:C], in_offset=None, bounds_check=N - 1, oob_is_err=False,
                    ).then_inc(s_wr[b], 16)

            tails(0, 0)
            tails(1, 1)

            def pair(i, static):
                for b in range(2):
                    tails(i * 2 + b + 2, b)
                    write(i * 2 + b, b)
            steps(pool, pair, NP2 - 1)
            write(NCH - 2, 0)
            write(NCH - 1, 1)
            for b in range(2):
                pool.wait_ge(s_wr[b], 16 * K * NP2)
            pool.wait_ge(s_si, 3)
            pool.indirect_dma_start(
                out=out, out_offset=bass.IndirectOffsetOnAxis(ap=seam_i[:, 4:5].bitcast(U32), axis=0),
                in_=rowO[:, 0, 0, 0:C], in_offset=None, bounds_check=N - 1, oob_is_err=False).then_inc(s_sw, 16)
            pool.wait_ge(s_sw, 48)

        @block.tensor
        def _(pe):
            te = nc.tensor
            pe.wait_ge(s_const, 15)

            def weights():
                pe.wait_ge(s_load, 16 * 10)
                pe.wait_ge(s_set, 11)
                te.matmul(psM[0:C, 0:R], w_sb[:, C:2 * C], relT[:, :], start=True, stop=True).then_inc(s_bc, 1)
                te.matmul(psM[0:C, R:2 * R], w_sb[:, 0:C], relT[:, :], start=True, stop=True).then_inc(s_bc, 1)
                te.matmul(psM[:, 2 * R:3 * R], bias_rep[:, :], relT[:, :], start=True, stop=True).then_inc(s_bc, 1)

            def transposes(row, n, parts, w, tr):
                for t in range(0, n, KT):
                    for k in range(t, min(t + KT, n)):
                        last = te.transpose(psT[0:w, t // KT, (k - t) * P:(k - t) * P + parts], row(k),
                                            ident[0:parts, 0:parts])
                    last.then_inc(tr, 1)

            def products(n, parts, w, pr):
                half = -(-n // 2)
                for k in range(n):
                    last = te.matmul(psP[0:parts, k // half, (k % half) * w:(k % half + 1) * w],
                                     vT[:, k * P:k * P + parts], V[:, 0:w], start=True, stop=True)
                last.then_inc(pr, 1)

            def node_transposes(j, b, i):
                pe.wait_ge(s_x[b], 32 * (i + 1))
                pe.sem_inc(s_turn_pe, 1)
                if not (isinstance(j, int) and j == 0):
                    pe.wait_ge(s_nb, j)
                    pe.sem_inc(s_turn_pe, 1)
                transposes(lambda k: xs[0:PN, b, k, :], KN, PN, C, s_ntr)

            def node_products(j):
                pe.wait_ge(s_ntc, j + 1)
                products(KN, PN, 3 * R, s_npr)

            for d in range(2):
                D = P if d == 0 else HI
                lhs = ident_h[:, :]

                vparts, aparts, nv, na = count_parts(d)
                v0, a0 = (d * NCH * count_parts(0)[n] for n in (2, 3))

                def count(i, static, D=D, vparts=vparts, aparts=aparts, nv=nv, na=na, v0=v0, a0=a0):
                    for q in range(Q):
                        j, parity = i * Q + q, q % 2
                        first_ = static and q == 0
                        for n in range(2):
                            for part_, b, made, done, base in (
                                    (vparts[n], 0, s_one, s_oned, v0 + j * nv - vparts[0][0]),
                                    (aparts[n], 1, s_sgn, s_sgnd, a0 + j * na - aparts[0][0])):
                                pe.wait_ge(made, base + part_[-1] + 1)
                                for k in part_:
                                    te.matmul(psR[b][:, 0:D], ident_h[:, :], rows_of[parity][:, k, 0:D],
                                              start=first_ and n == 0 and k == part_[0], stop=True,
                                              skip_group_check=True).then_inc(done, 1)
                steps(pe, count, NCH // Q)
                pe.wait_ge(s_tot, d + 1)
                te.matmul(psR[0][:, 0:D], before[:, :], counts[:, 0:D], start=True, stop=True)
                te.matmul(psR[1][:, 0:D], ones[:, :], counts[:, 0:D], start=True, stop=True).then_inc(s_base, 1)
                if d == 0:
                    weights()
                    pe.wait_ge(s_mat, 1)
                pe.wait_ge(s_basep, d + 1)
                te.matmul(psR[0][:, 0:D], ident[:, :], counts[:, 0:D], start=True, stop=True)
                te.matmul(psR[1][:, 0:D], ident[:, :], counts[:, 0:D], start=True, stop=True).then_inc(s_base, 1)

                def add(j, static, meanwhile=None, d=d, D=D):
                    def into(b, g):
                        for k in range(g * G, (g + 1) * G):
                            te.matmul(psR[b][:, 0:D], lhs, onehot[:, k, 0:D], start=False, stop=True,
                                      skip_group_check=True).then_inc(s_cnt, 1)

                    def heads(g):
                        for n in range(g * G, (g + 1) * G):
                            te.matmul(psM[:, 0:HI], onehot2[:, n, :], onehot[:, n, :],
                                      start=static and n == 0, stop=True, skip_group_check=True)
                    if meanwhile:
                        meanwhile[0]()
                    for g in range(2):
                        pe.wait_ge(s_hot, d * T + j * K + (g + 1) * G)
                        into(1 - g, g)
                        if d == 1:
                            heads(g)
                        if g == 0 and meanwhile:
                            meanwhile[1]()
                        pe.wait_ge(s_read, d * T + j * K + (g + 1) * G)
                        into(g, g)
                if d == 0:
                    def with_nodes(i, static):
                        for b in range(2):
                            n = i * 2 + b
                            add(n + LAG, False, (lambda: node_transposes(n, b, i), lambda: node_products(n)))
                    for j in range(LAG):
                        add(j, False)
                    steps(pe, with_nodes, NN2)
                    n = NCN - 1
                    add(n + LAG, False, (lambda: node_transposes(n, 0, NN2), lambda: node_products(n)))
                    for j in range(NCN + LAG, NCH):
                        add(j, False)
                else:
                    steps(pe, add, NCH)
            pe.wait_ge(s_map, 1)
            te.matmul(psR[0][:, 0:HI], upto_p[:, :], counts[:, :], start=True, stop=True).then_inc(s_mapd, 1)

            for n in range(3):
                pe.wait_ge(s_mat, 1 + n + 1)
                te.matmul(psM[:, n * P:(n + 1) * P], ones[:, :], dg[:, n % 2, :], start=True, stop=True).then_inc(s_bc, 1)

            def look(j):
                pe.wait_ge(s_lo, j + 1)
                pe.sem_inc(s_turn_pe, 1)
                for t in range(0, K, KT):
                    for k in range(t, min(t + KT, K)):
                        last = te.matmul(psT[:, t // KT, (k - t) * P:(k - t + 1) * P], lot[:, k, :], ident_h[:, :],
                                         start=True, stop=True)
                    last.then_inc(s_lt, 1)
                pe.wait_ge(s_ltc, j + 1)
                if not (isinstance(j, int) and j == 0):
                    pe.wait_ge(s_took, j * K)
                    if not (isinstance(j, int) and j == 1):
                        pe.wait_ge(s_out, j - 1)
                for k in range(K):
                    if k >= 4:
                        pe.wait_ge(s_took, j * K + k - 3)
                    for n in range(2):
                        last = te.matmul(psL[k % 4][:, 0:HI], lotT[:, k * P:(k + 1) * P], row_p[:, n, :],
                                         start=n == 0, stop=n == 1)
                    last.then_inc(s_look, 1)

            def project(j, b, looked):
                pe.wait_ge(s_v, j + 1)
                pe.sem_inc(s_turn_pe, 1)
                transposes(lambda k: rowO[:, b, k, 0:CO], K, P, CO, s_tr)
                pe.wait_ge(s_trc, j + 1)
                pe.wait_ge(s_took, looked * K)
                if not (isinstance(j, int) and j == 0):
                    pe.wait_ge(s_out, j)
                products(K, P, 2 * R, s_pr)

            def chunk(i, static):
                for b in range(2):
                    look(i * 2 + b + 1)
                    project(i * 2 + b, b, i * 2 + b + 2)
            look(0)
            steps(pe, chunk, NP2 - 1)
            look(NCH - 1)
            project(NCH - 2, 0, NCH)
            project(NCH - 1, 1, NCH)

            for h in range(2):
                pe.wait_ge(s_mat, 4 + 3 * h + 1)
                te.matmul(psM[:, 0:P], ones[:, :], dg[:, 0, :], start=True, stop=True).then_inc(s_bc, 1)
                pe.wait_ge(s_mat, 4 + 3 * h + 2)
                te.transpose(psM[:, P:2 * P], sx[:, :], ident[:, :]).then_inc(s_bc, 1)
                pe.wait_ge(s_mat, 4 + 3 * h + 3)
                te.matmul(psR[0][:, 0:CO], sxT[:, :], S[:, :, K], start=True, stop=True).then_inc(s_bc, 1)
                if h == 0:
                    pe.wait_ge(s_v, NCH + 1)
                    pe.sem_inc(s_turn_pe, 1)
                    transposes(lambda k: rowO[:, 0, k, 0:CO], 1, P, CO, s_tr)
                    pe.wait_ge(s_trc, NCH + 1)
                    pe.wait_ge(s_out, NCH)
                    products(1, P, 2 * R, s_pr)

        @block.scalar
        def _(act):
            sc_ = nc.scalar
            act.wait_ge(s_const, 15)

            def copies(tr, done, out_sem, n, w, parts, link_sem, rows):
                nb = -(-n // KT)
                for t in range(nb):
                    k0, k1 = t * KT, min((t + 1) * KT, n)
                    act.wait_ge(tr, done + t + 1)
                    o = w[0:rows, k0 * P:k1 * P].rearrange("p (k q) -> p k q", q=P)[:, :, 0:parts]
                    i = psT[0:rows, t, 0:(k1 - k0) * P].rearrange("p (k q) -> p k q", q=P)[:, :, 0:parts]
                    sc_.copy(o, i).then_inc(out_sem if t == nb - 1 else link_sem, 1)

            NB, NBN = -(-K // KT), -(-KN // KT)

            def node(j, b, i):
                copies(s_ntr, j * NBN, s_ntc, KN, vT, PN, s_act, C)
                act.wait_ge(s_cen, j + 1)
                sc_.activation(nsq[0:PN, :, :], xc[0:PN, :, :], ACT.Square).then_inc(s_nsq, 1)
                act.wait_ge(s_nroot, 2 * j + 1)
                sc_.activation(ns[0:PN, 2, :], ns[0:PN, 0, :], ACT.Sqrt).then_inc(s_nrt, 1)
                act.wait_ge(s_x[b], 32 * (i + 1))
                if not (isinstance(j, int) and j < 2):
                    act.wait_ge(s_nst[b], NST * i)
                for to in (nT, nH):
                    sc_.copy(to[0:PN, b, :, 0:C], xs[0:PN, b, :, :]).then_inc(s_act, 1)
                act.wait_ge(s_npr, j + 1)
                pr = psP[0:PN, :, 0:KN // 2 * 3 * R].rearrange("p n (k r) -> p n k r", r=3 * R)
                if not (isinstance(j, int) and j == 0):
                    act.wait_ge(s_node, j)
                for n, to in ((2, nB[0:PN]), (0, nT[0:PN, b, :, B0:B0 + R].rearrange("p (n k) r -> p n k r", n=2)),
                              (1, nH[0:PN, b, :, C:WH].rearrange("p (n k) r -> p n k r", n=2))):
                    sc_.copy(to, pr[:, :, :, n * R:(n + 1) * R]).then_inc(s_nb if n == 1 else s_act, 1)
                act.wait_ge(s_nroot, 2 * j + 2)
                sc_.activation(ns[0:PN, 3, :], ns[0:PN, 1, :], ACT.Sqrt, bias=eps[0:PN, :], scale=1.0 / C).then_inc(s_nrt, 1)
                act.wait_ge(s_nr, j + 1)
                for k in range(KN):
                    last = sc_.activation(n1[0:PN, b, k, 0:C], xs[0:PN, b, k, :], ACT.Copy, scale=ns[0:PN, 5, k:k + 1])
                last.then_inc(s_nact, 1)
            def signs_of(d):
                D = (P, HI)[d]
                parts_, na, base = count_parts(d)[1], count_parts(d)[3], d * NCH * count_parts(0)[3]
                act.wait_ge(s_half, d + 1)

                def rows(i, static):
                    for q in range(Q):
                        j, parity = i * Q + q, q % 2
                        for part_ in parts_:
                            if not (static and q < 2):
                                act.wait_ge(s_sgnd, base + (j - 2) * na + part_[-1] + 1 - parts_[0][0])
                            for k in part_:
                                sc_.activation(rows_of[parity][:, k, 0:D], iota_h[:, 0:D], ACT.Sign,
                                               bias=half_less[:, bass.ds(j * K + k, 1)]).then_inc(s_sgn, 1)
                steps(act, rows, NCH // Q)

            signs_of(0)

            def nodes(i, static):
                node(i * 2, 0, i)
                node(i * 2 + 1, 1, i)
            steps(act, nodes, NN2)
            node(NCN - 1, 0, NN2)
            signs_of(1)
            act0 = NCN * (3 + NBN)

            for h in range(2):
                nr = 1 + h
                r0 = (0, NCH + 1)[h]
                e0, x0 = h * (NCH + 1), h * (NCH + 1)
                per = (1 + 2 * (NB - 1), 1)[h]
                a0 = (act0 + NB - 1, act0 + NCH * (1 + 2 * (NB - 1)))[h]
                if h == 0:
                    copies(s_lt, 0, s_ltc, K, lotT, P, s_act, P)

                def chunk(j, b, static, i, ahead=True, h=h, nr=nr, r0=r0, e0=e0, per=per, a0=a0):
                    if h == 0 and ahead:
                        copies(s_lt, (j + 1) * NB, s_ltc, K, lotT, P, s_act, P)
                    act.wait_ge(s_dl, e0 + j + 1)
                    sc_.activation(ex[:, :, :], dl[:, :, :], ACT.Exp).then_inc(s_act, 1)
                    act.wait_ge(s_act, a0 + j * per + (NB if h == 0 and ahead else 1))
                    sc_.copy(decay[:, :, 1:K + 1], ex[:, 0:1, :].to_broadcast([P, CO, K])).then_inc(s_ex, 1)
                    if h == 0:
                        if not (static and i == 0):
                            act.wait_ge(s_dump[b], 32 * i)
                        sc_.copy(rowO[:, b, :, X0:W1], rowH[:, b, :, 0:C]).then_inc(s_xc, 1)
                    for n in range(nr):
                        act.wait_ge(s_sq, r0 + j * nr + n + 1)
                        sc_.activation(sq[:, :, :], v[:, :, :], ACT.Square).then_inc(s_sqd, 1)
                        act.wait_ge(s_ask, r0 + j * nr + n + 1)
                        sc_.activation(rs[:, :], ss[:, :], ACT.Sqrt).then_inc(s_rt, 1)
                    if h == 0:
                        copies(s_tr, j * NB, s_trc, K, vT, P, s_act, CO)
                        act.wait_ge(s_pr, j + 1)
                        sc_.copy(rowO[:, b, :, B0:X0].rearrange("p (n k) r -> p n k r", n=2),
                                 psP[:, :, 0:K // 2 * 2 * R].rearrange("p n (k r) -> p n k r", r=2 * R)).then_inc(s_out, 1)

                def pair(i, static, chunk=chunk):
                    chunk(i * 2, 0, static, i)
                    chunk(i * 2 + 1, 1, static, i)
                steps(act, pair, NP2 - 1)
                chunk(NCH - 2, 0, False, NP2 - 1)
                chunk(NCH - 1, 1, False, NP2 - 1, False)
                act.wait_ge(s_dl, e0 + NCH + 1)
                sc_.activation(sx[:, :], mm[:, :], ACT.Exp, bias=sv[:, 2:3]).then_inc(s_mat, 1)
                sc_.activation(sv[:, 4:5], sv[:, 3:4], ACT.Exp).then_inc(s_ex, 1)
                if h == 0:
                    act.wait_ge(s_sg, 16)
                    act.wait_ge(s_dump[0], 32 * NP2)
                    sc_.copy(rowO[:, 0, 0, X0:W1], seam_row[:, 0:C]).then_inc(s_xc, 1)
                for n in range(nr):
                    act.wait_ge(s_sq, r0 + NCH * nr + n + 1)
                    sc_.activation(sq[:, 0:1, :], v[:, 0:1, :], ACT.Square).then_inc(s_sqd, 1)
                    act.wait_ge(s_ask, r0 + NCH * nr + n + 1)
                    sc_.activation(rs[:, 0:1], ss[:, 0:1], ACT.Sqrt).then_inc(s_rt, 1)
                if h == 0:
                    copies(s_tr, NCH * NB, s_trc, 1, vT, P, s_act, CO)
                    act.wait_ge(s_pr, NCH + 1)
                    sc_.copy(rowO[:, 0, 0, B0:X0], psP[:, 0, 0:2 * R]).then_inc(s_out, 1)

        @block.vector
        def _(dve):
            ve = nc.vector
            link = Link(dve, s_dve)

            def wide(a, n=K, c=C, p=P):
                return a.unsqueeze(2).to_broadcast([p, n, c])

            dve.wait_ge(s_const, 15)
            link(ve.tensor_copy(iota_h[:, :], iota_i[:, :]))
            link(ve.tensor_copy(ident_h[:, :], ident[:, :]))
            dve.wait_ge(s_src, 32)

            def take_weights():
                dve.wait_ge(s_set, 11)
                dve.wait_ge(s_bc, 3)
                link(ve.tensor_copy(V[0:C, 0:2 * R], psM[0:C, 0:2 * R]))
                link(ve.tensor_copy(V[0:C, 2 * R:3 * R], psM[0:C, 0:R]))
                link(ve.tensor_copy(V[C:CO, 0:R], psM[C:CO, 2 * R:3 * R]))
                ve.tensor_copy(brel[:, :], psM[:, 2 * R:3 * R]).then_inc(s_mat, 1)

            ss_, w, nrm, dev, ssv, r, m, m2, s, t = (ns[0:PN, n, :] for n in range(10))

            def node_centre(j, b, i, meanwhile):
                X = xs[0:PN, b, :, :]
                dve.wait_ge(s_x[b], 32 * (i + 1))
                if not (isinstance(j, int) and j < 2):
                    dve.wait_ge(s_nst[b], NST * i)
                link(ve.tensor_reduce(m, X, AX.X, ALU.add), meanwhile)
                ve.scalar_tensor_tensor(xc[0:PN, :, :], wide(m, KN, C, PN), 1.0 / C, X, ALU.mult, ALU.subtract).then_inc(s_cen, 1)
                link(ve.tensor_tensor(m2, m, m, ALU.mult))

            def node_squares(j, meanwhile):
                dve.wait_ge(s_nsq, j + 1)
                link(ve.tensor_reduce(ssv, nsq[0:PN, :, :], AX.X, ALU.add), meanwhile)
                ve.scalar_tensor_tensor(ss_, m2, 1.0 / C, ssv, ALU.mult, ALU.add).then_inc(s_nroot, 1)

            def node_scales(j, bank_ready, pick):
                dve.wait_ge(s_nrt, 2 * j + 1)
                link(ve.tensor_scalar(r, nrm, 1e-12, None, ALU.max), bank_ready)
                link(ve.reciprocal(r, r), lambda: pick(G))
                ve.tensor_tensor(t, nrm, r, ALU.mult).then_inc(s_nr, 1)
                pick(G + 1)
                dve.wait_ge(s_nr, j + 1)
                link(ve.tensor_scalar(t, t, 1e-12, None, ALU.max), lambda: pick(G + 2))
                link(ve.reciprocal(t, t), lambda: pick(G + 3))
                link(ve.tensor_tensor(s, r, t, ALU.mult), lambda: pick(G + 4))
                link(ve.tensor_scalar(s, s, 1.0, None, ALU.add), lambda: pick(G + 5))
                link(ve.tensor_tensor(t, s, s, ALU.mult), lambda: pick(G + 6))
                ve.tensor_tensor(w, t, ssv, ALU.mult).then_inc(s_nroot, 1)

            def node_rows(j, b):
                dve.wait_ge(s_nb, j + 1)
                n1B = n1[0:PN, b, :, B0:B0 + R]
                link(ve.tensor_tensor(n1B.rearrange("p (n k) r -> p n k r", n=2), nB[0:PN, :, :, :],
                                      r.rearrange("p (n k) -> p n k", n=2).unsqueeze(3).to_broadcast([PN, 2, KN // 2, R]), ALU.mult))
                ve.tensor_tensor(n1B, n1B, brel[0:PN, :].unsqueeze(1).to_broadcast([PN, KN, R]), ALU.add)
                dve.wait_ge(s_nrt, 2 * j + 2)
                link(ve.reciprocal(dev, dev))
                link(ve.scalar_tensor_tensor(t, s, -1.0, dev, ALU.mult, ALU.mult))
                ve.tensor_tensor(nout[0:PN, b, :, :], xc[0:PN, :, :], wide(t, KN, C, PN), ALU.mult).then_inc(s_node, 1)

            for d in range(2):
                D = P if d == 0 else HI
                lead = (LAG, 6)[d]
                if d == 1:
                    dve.wait_ge(s_cnt, 2 * T)
                    dve.wait_ge(s_again, 16)
                    link(ve.tensor_scalar(dig_i[:, :], edges[:, :, 0], P - 1, None, ALU.bitwise_and))
                    link(ve.tensor_copy(dig2[:, :], dig_i[:, :]))
                    link(ve.tensor_scalar(dig_i[:, :], edges[:, :, 0], 7, None, ALU.logical_shift_right))
                else:
                    link(ve.tensor_scalar(dig_i[:, :], raw[:, 0, :], P - 1, None, ALU.bitwise_and))
                link(ve.tensor_copy(dig[:, :], dig_i[:, :]))
                ve.tensor_scalar(half_less[:, :], dig[:, :], -1.0, 0.5, ALU.mult, ALU.add).then_inc(s_half, 1)
                vparts, _, nv, na = count_parts(d)
                vbase, abase = (d * NCH * count_parts(0)[n] for n in (2, 3))

                def hot(j, k, made, rows=onehot, D=D):
                    ve.tensor_scalar(rows[:, k, 0:D], iota_h[:, 0:D], dig[:, bass.ds(j * K + k, 1)], None,
                                     ALU.is_equal).then_inc(made, 1)

                def count(i, static, vparts=vparts, nv=nv, vbase=vbase, hot=hot):
                    for q in range(Q):
                        j, parity = i * Q + q, q % 2
                        for part_ in vparts:
                            if not (static and q < 2):
                                dve.wait_ge(s_oned, vbase + (j - 2) * nv + part_[-1] + 1)
                            for k in part_:
                                hot(j, k, s_one, rows_of[parity])
                steps(dve, count, NCH // Q)
                n1_ = d * 2 * T

                def prior_of(j0, j1):
                    cc = slice(j0 * K, j1 * K)
                    digs = dig[:, cc].rearrange("p (n a) -> p n a", a=G)
                    groups = (P, (j1 - j0) * 2, G, G)
                    eq = same[:, 2 * j0:2 * j1, :, :]
                    link(ve.tensor_tensor(eq, digs.unsqueeze(3).to_broadcast(list(groups)),
                                          digs.unsqueeze(2).to_broadcast(list(groups)), ALU.is_equal))
                    link(ve.tensor_tensor(eq, eq, tri[:, :, :].unsqueeze(1).to_broadcast(list(groups)), ALU.mult))
                    link(ve.tensor_reduce(prior[:, cc].rearrange("p (n a) -> p n a", a=G), eq, AX.X, ALU.add))

                def hots(j, g, group, d=d, n1_=n1_, hot=hot):
                    if group[0] % G == 0 and not (isinstance(j, int) and j == 0):
                        dve.wait_ge(s_cnt, n1_ + 2 * (j - 1) * K + 2 * (g + 1) * G)
                    for k in group:
                        if d == 1:
                            ve.tensor_scalar(onehot2[:, k, :], iota_h[:, 0:P], dig2[:, bass.ds(j * K + k, 1)], None,
                                             ALU.is_equal)
                        hot(j, k, s_hot)

                def bank_ready(j, g, d=d, n1_=n1_):
                    dve.wait_ge(s_hot, d * T + j * K + (g + 1) * G)
                    if not (isinstance(j, int) and j == 0 and d == 0 and g == 0):
                        dve.wait_ge(s_read, d * T + j * K + g * G)
                    if not (isinstance(j, int) and j == 0 and d == 0 and g == 0):
                        dve.wait_ge(s_cnt, n1_ + 2 * j * K + (-G if g == 0 else G))

                def pick(k, D=D):
                    ve.tensor_tensor_reduce(out=picks[:, k % G, 0:D], in0=onehot[:, k, 0:D], in1=psR[k // G][:, 0:D],
                                            scale=1.0, scalar=0.0, op0=ALU.mult, op1=ALU.add,
                                            accum_out=rank[:, k:k + 1]).then_inc(s_read, 1)

                def put_up(j, b, i, early, d=d):
                    dve.wait_ge(s_read, d * T + (j + 1) * K)
                    if not early:
                        dve.wait_ge(s_sct[b], 16 * K * (d * NP2 + i))
                    link(ve.tensor_tensor(place[:, b, :], rank[:, :], prior[:, cols(j)], ALU.add))
                    ve.tensor_copy(moved[:, b, :, :], edges[:, cols(j), :]).then_inc(s_plc, 1)

                def ranks(j, b, i, early=False, hot_made=False, hots=hots, bank_ready=bank_ready, pick=pick, put_up=put_up):
                    for g in range(2):
                        group = range(g * G, (g + 1) * G)
                        if not hot_made:
                            hots(j, g, group)
                        bank_ready(j, g)
                        for k in group:
                            pick(k)
                    put_up(j, b, i, early)

                def with_nodes(n, b, i, hots=hots, bank_ready=bank_ready, pick=pick, put_up=put_up):
                    j = n + LAG
                    node_centre(n, b, i, lambda: hots(j, 0, range(G)))
                    bank_ready(j, 0)
                    for k in range(G):
                        pick(k)
                    node_squares(n, lambda: hots(j, 1, range(G, G + 1)))
                    hots(j, 1, range(G + 1, K))
                    node_scales(n, lambda: bank_ready(j, 1), pick)
                    put_up(j, b, i + LAG // 2, False)
                    node_rows(n, b)

                dve.wait_ge(s_oned, vbase + (NCH - 1) * nv)
                dve.wait_ge(s_sgnd, abase + (NCH - 1) * na)
                for g in range(2):
                    hots(0, g, range(g * G, (g + 1) * G))
                dve.wait_ge(s_oned, vbase + NCH * nv)
                dve.wait_ge(s_sgnd, abase + NCH * na)
                link(ve.memset(signs[:, 0:1], -float(NCH * na)))
                link(ve.tensor_copy(signs[:, 1:D + 1], psR[1][:, 0:D]))
                link(ve.tensor_tensor(totals[:, 0:D], signs[:, 1:D + 1], signs[:, 0:D], ALU.subtract))
                ve.scalar_tensor_tensor(counts[:, 0:D], totals[:, 0:D], 0.5, psR[0][:, 0:D], ALU.mult, ALU.add).then_inc(s_tot, 1)
                prior_of(0, lead)
                dve.wait_ge(s_base, 2 * d + 1)
                link(ve.tensor_copy(totals[:, 0:D], psR[1][:, 0:D]))
                link(ve.tensor_tensor_scan(starts[:, 0:D], zeros[:, 0:D], totals[:, 0:D], 0.0, ALU.add, ALU.add))
                link(ve.tensor_tensor(starts[:, 0:D], starts[:, 0:D], totals[:, 0:D], ALU.subtract))
                ve.tensor_tensor(counts[:, 0:D], starts[:, 0:D], psR[0][:, 0:D], ALU.add).then_inc(s_basep, 1)
                if d == 0:
                    take_weights()
                dve.wait_ge(s_base, 2 * d + 2)
                for j in range(lead):
                    ranks(j, j % 2, j // 2, d == 0, j == 0)
                prior_of(lead, NCH)
                if d == 0:
                    def pair(i, static):
                        link.enter(i, 2 * 14)
                        for b in range(2):
                            with_nodes(i * 2 + b, b, i)
                    link.base += link.n
                    steps(dve, pair, NN2)
                    link.leave(NN2)
                    with_nodes(NCN - 1, 0, NN2)
                    for j in range(NCN + LAG, NCH):
                        ranks(j, j % 2, j // 2)
                else:
                    def pair(i, static, ranks=ranks, lead=lead):
                        link.enter(i, 2)
                        for b in range(2):
                            ranks(i * 2 + b + lead, b, i + lead // 2)
                    link.base += link.n
                    steps(dve, pair, NP2 - lead // 2)
                    link.leave(NP2 - lead // 2)

            dve.wait_ge(s_cnt, 4 * T)
            ve.tensor_copy(counts[:, :], psM[:, 0:HI]).then_inc(s_map, 1)
            dve.wait_ge(s_mapd, 1)
            link(ve.tensor_tensor(row_of[:, :], starts[:, :], psR[0][:, 0:HI], ALU.add))
            link(ve.tensor_scalar(row_of[:, :], row_of[:, :], -1.0, None, ALU.add))
            link(ve.tensor_tensor(totals[:, :], node_f[:, :], row_of[:, :], ALU.subtract))
            link(ve.tensor_scalar(starts[:, :], counts[:, :], 0.0, None, ALU.is_equal))
            link(ve.tensor_tensor(totals[:, :], totals[:, :], starts[:, :], ALU.mult))
            link(ve.tensor_tensor(row_of[:, :], row_of[:, :], totals[:, :], ALU.add))
            link(ve.tensor_copy(row_i[:, :], row_of[:, :]))
            link(ve.tensor_scalar(part_i[:, :], row_i[:, :], 511, None, ALU.bitwise_and))
            link(ve.tensor_scalar(row_p[:, 1, :], part_i[:, :], 0.25, None, ALU.mult))
            link(ve.tensor_scalar(row_i[:, :], row_i[:, :], 9, None, ALU.logical_shift_right))
            link(ve.tensor_scalar(row_p[:, 0, :], row_i[:, :], 128.0, None, ALU.mult))

            dve.wait_ge(s_again, 48)

            def indices(j, b, h):
                if h == 0:
                    link(ve.tensor_copy(gi[:, b, 0, :], edges[:, cols(j), 0]))
                    ve.tensor_copy(gi[:, b, 1, :], edges[:, cols(j), 1]).then_inc(s_idx, 1)
                else:
                    ve.tensor_copy(gi[:, b, 1, :], tail_row[:, cols(j)]).then_inc(s_idx, 1)

            indices(0, 0, 0)
            indices(1, 1, 0)
            link(ve.tensor_copy(head_f[:, :], edges[:, :, 0]))
            link(ve.tensor_copy(type_f[:, :], edges[:, :, 2]))
            link(ve.tensor_scalar(dig_i[:, :], edges[:, :, 1], P - 1, None, ALU.bitwise_and))
            link(ve.tensor_copy(dig2[:, :], dig_i[:, :]))
            link(ve.tensor_scalar(dig_i[:, :], edges[:, :, 1], 7, None, ALU.logical_shift_right))
            link(ve.tensor_copy(dig[:, :], dig_i[:, :]))
            link(ve.memset(differ[:, 0:1], 1.0))
            link(ve.tensor_tensor(differ[:, 1:T], head_f[:, 1:T], head_f[:, 0:T - 1], ALU.not_equal))
            link(ve.tensor_copy(is_end[:, 0:T - 1], differ[:, 1:T]))
            link(ve.tensor_copy(sv[:, 0:1], next_head[:, 0:1]))
            link(ve.tensor_tensor(is_end[:, T - 1:T], head_f[:, T - 1:T], sv[:, 0:1], ALU.not_equal))
            link(ve.tensor_scalar(not_end[:, :], is_end[:, :], -1.0, 1.0, ALU.mult, ALU.add))
            link(ve.tensor_scalar(cut[:, :], differ[:, :], -BIG, None, ALU.mult))
            link(ve.tensor_scalar(differ[:, :], differ[:, :], -1.0, 1.0, ALU.mult, ALU.add))
            link(ve.memset(differ[:, 0:1], 1.0))
            link(ve.tensor_tensor_scan(in_first[:, :], differ[:, :], zeros[:, 0:T], 1.0, ALU.mult, ALU.add))
            link(ve.tensor_tensor(first_end[:, :], in_first[:, :], is_end[:, :], ALU.mult))
            link(ve.tensor_tensor(mid_end[:, :], is_end[:, :], first_end[:, :], ALU.subtract))
            link(ve.tensor_scalar(write_f[:, :], is_end[:, :], -FAR, FAR, ALU.mult, ALU.add))
            link(ve.tensor_tensor(write_f[:, :], write_f[:, :], head_f[:, :], ALU.add))

            link(ve.tensor_tensor_scan(in_last[:, ::-1], not_end[:, ::-1], zeros[:, 0:T], 1.0, ALU.mult, ALU.add))
            fh, lh, mF, mL = head_f[:, 0:1], head_f[:, T - 1:T], first[:, CO:CO + 1], mb[:, K:K + 1]
            link(ve.tensor_reduce(sv[:, 1:2], first_end[:, :], AX.X, ALU.max))
            link(ve.tensor_reduce(sv[:, 5:6], in_first[:, :], AX.X, ALU.add))
            link(ve.tensor_tensor(sv[:, 5:6], sv[:, 5:6], spot_f[:, :], ALU.add))
            link(ve.tensor_scalar(sv[:, 6:7], sv[:, 1:2], -FAR, FAR, ALU.mult, ALU.add))
            link(ve.tensor_tensor(sv[:, 7:8], sv[:, 6:7], sv[:, 5:6], ALU.add))
            link(ve.tensor_tensor(sv[:, 8:9], sv[:, 6:7], fh, ALU.add))
            link(ve.tensor_scalar(in_first[:, :], in_first[:, :], sv[:, 1:2], None, ALU.mult))
            for n, a in enumerate((lh, fh, sv[:, 5:6])):
                if n == 2:
                    dve.wait_ge(s_bc, 4)
                ve.tensor_scalar(dg[:, n % 2, :], ident[:, :], a, None, ALU.mult).then_inc(s_mat, 1)
            dve.wait_ge(s_bc, 6)
            link(ve.tensor_scalar(earlier, psM[:, 0:P], fh, None, ALU.is_equal))
            link(ve.tensor_tensor(earlier, earlier, after[:, :], ALU.mult))
            link(ve.tensor_scalar(not_earlier, earlier, BIG, -BIG, ALU.mult, ALU.add))
            link(ve.tensor_scalar(wt[:, :], psM[:, P:2 * P], lh, None, ALU.is_equal))
            link(ve.tensor_tensor(wt[:, :], wt[:, :], before[:, :], ALU.mult))
            link(ve.tensor_tensor(mm[:, :], wt[:, :], psM[:, 2 * P:3 * P], ALU.mult))
            link(ve.tensor_reduce(sv[:, 9:10], mm[:, :], AX.X, ALU.max))
            for n, a in enumerate((fh, sv[:, 7:8], sv[:, 9:10], sv[:, 5:6])):
                link(ve.tensor_copy(seam_i[:, n:n + 1], a))
            ve.tensor_copy(seam_i[:, 4:5], sv[:, 8:9]).then_inc(s_si, 1)

            def finish_norm(K0, root):
                dve.wait_ge(s_sqd, root)
                ve.tensor_reduce(ss[:, 0:K0], sq[:, 0:K0, :], AX.X, ALU.add).then_inc(s_ask, 1)
                dve.wait_ge(s_rt, root)
                link(ve.tensor_scalar(rs[:, 0:K0], rs[:, 0:K0], 1e-12, None, ALU.max))
                link(ve.reciprocal(rs[:, 0:K0], rs[:, 0:K0]))

            def finish(h, K0, b, rowsH, root, pr, agg, meanwhile, free):
                vv = v[:, 0:K0, :]
                link(ve.tensor_tensor(vv, agg, wide(rd[:, 0:K0], K0), ALU.mult))
                ve.tensor_tensor(vv, vv, rowsH[:, :, 0:C], ALU.add).then_inc(s_sq, 1)
                if h == 0:
                    free()
                meanwhile[0]()
                finish_norm(K0, root + 1)
                if h == 0:
                    ve.tensor_tensor(rowO[:, b, 0:K0, 0:C], vv, wide(rs[:, 0:K0], K0), ALU.mult).then_inc(s_v, 1)
                    meanwhile[1]()
                    if K0 == 1:
                        dve.wait_ge(s_out, pr)
                else:
                    link(ve.tensor_tensor(vv, vv, wide(rs[:, 0:K0], K0), ALU.mult))
                    link(ve.tensor_tensor(vv, vv, rowsH[:, :, X0:W1], ALU.add))
                    free()
                    link(ve.tensor_reduce(mean[:, 0:K0], vv, AX.X, ALU.add))
                    link(ve.tensor_scalar(mean[:, 0:K0], mean[:, 0:K0], 1.0 / C, None, ALU.mult))
                    ve.tensor_tensor(vv, vv, wide(mean[:, 0:K0], K0), ALU.subtract).then_inc(s_sq, 1)
                    meanwhile[1]()
                    dve.wait_ge(s_sqd, root + 2)
                    link(ve.tensor_reduce(ss[:, 0:K0], sq[:, 0:K0, :], AX.X, ALU.add))
                    ve.tensor_scalar(ss[:, 0:K0], ss[:, 0:K0], 1.0 / C, 1e-5, ALU.mult, ALU.add).then_inc(s_ask, 1)
                    dve.wait_ge(s_rt, root + 2)
                    link(ve.reciprocal(rs[:, 0:K0], rs[:, 0:K0]))
                    link(ve.tensor_tensor(rowO[:, b, 0:K0, 0:C], vv, wide(rs[:, 0:K0], K0), ALU.mult))

            def nothing():
                pass

            def keep_A(j, b):
                dve.wait_ge(s_out, j + 1)
                ve.tensor_tensor(AE[:, :, cols(j)], rowO[:, b, :, A0:A0 + R].rearrange("p k r -> p r k"),
                                 mid_end[:, cols(j)].unsqueeze(1).to_broadcast([P, R, K]), ALU.mult).then_inc(s_kept, 1)

            def spread_A(r0_, r1_):
                for r_ in range(r0_, r1_):
                    ve.tensor_tensor_scan(AE[:, r_, ::-1], not_end[:, ::-1], AE[:, r_, ::-1], 0.0,
                                          ALU.mult, ALU.add).then_inc(s_spread, 1)

            PER = (21, 30)
            for h in range(2):
                nr, r0, e0, x0 = 1 + h, (0, NCH + 1)[h], h * (NCH + 1), h * (NCH + 1)
                link(ve.memset(mb, -BIG))
                link(ve.memset(S[:, :, :], 0.0))
                link(ve.memset(first[:, :], 0.0))

                def lows(j, ks):
                    for k in ks:
                        hot = ve.tensor_scalar(lot[:, k, :], iota_h[:, 0:P], dig2[:, bass.ds(j * K + k, 1)], None, ALU.is_equal)
                        if k == K - 1:
                            hot.then_inc(s_lo, 1)

                def highs(j, ks):
                    for k in ks:
                        ve.tensor_scalar(onehot[:, k, :], iota_h[:, :], dig[:, bass.ds(j * K + k, 1)], None,
                                         ALU.is_equal).then_inc(s_hot, 1)

                def take_rows(j):
                    dve.wait_ge(s_hot, 2 * T + (j + 1) * K)
                    for k in range(K):
                        dve.wait_ge(s_look, j * K + k + 1)
                        if k >= 4:
                            dve.wait_ge(s_took, j * K + k - 3)
                        ve.tensor_tensor_reduce(out=picked[:, k % 4, :], in0=onehot[:, k, :], in1=psL[k % 4][:, 0:HI],
                                                scale=4.0, scalar=0.0, op0=ALU.mult, op1=ALU.add,
                                                accum_out=rank[:, k:k + 1]).then_inc(s_took, 1)
                    dve.wait_ge(s_took, (j + 1) * K)
                    link(ve.tensor_copy(tail_row[:, cols(j)], rank[:, :]))

                if h == 0:
                    lows(0, range(K))
                    highs(0, range(K))
                    take_rows(0)

                def chunk(j, b, static, ahead, i, more=h == 0, h=h, nr=nr, r0=r0, e0=e0, x0=x0):
                    cc = cols(j)
                    H, Tl = rowH[:, b, :, :], rowT[:, b, :, :]
                    if more:
                        lows(j + 1, range(0, 2))
                    def high(k):
                        return (lambda: highs(j + 1, range(k, k + 1))) if more else None

                    def low(k):
                        return (lambda: lows(j + 1, range(k, k + 2))) if more else None
                    link(ve.tensor_tensor(typ[:, :, :], iota_r[:, :].unsqueeze(1).to_broadcast([P, K, R]),
                                          wide(type_f[:, cc], K, R), ALU.is_equal), low(2))
                    if h == 0:
                        dve.wait_ge(s_gat[b], 16 * 2 * K * (i + 1))
                        link(ve.tensor_tensor(sc[:, :, :], H[:, :, C:C + R], Tl[:, :, B0:B0 + R], ALU.add), low(4))
                    else:
                        fa, la = (cap[:, n * R:(n + 1) * R, :].rearrange("p r k -> p k r") for n in range(2))
                        last_A = last_row[:, A0:A0 + R]
                        link(ve.tensor_tensor(fa, first_A.unsqueeze(1).to_broadcast([P, K, R]), wide(in_first[:, cc], K, R), ALU.mult))
                        link(ve.tensor_tensor(la, last_A.unsqueeze(1).to_broadcast([P, K, R]), wide(in_last[:, cc], K, R), ALU.mult))
                        link(ve.tensor_tensor(fa, fa, la, ALU.add))
                        link(ve.tensor_tensor(fa, fa, AE[:, :, cc].rearrange("p r k -> p k r"), ALU.add))
                        dve.wait_ge(s_gat[b], 16 * K * (2 * NP2 + i + 1))
                        dve.wait_ge(s_hl[b], 16 * (i + 1))
                        link(ve.tensor_tensor(sc[:, :, :], fa,
                                              Tl[:, :, B0:B0 + R], ALU.add))
                    link(ve.tensor_tensor(sc[:, :, :], sc[:, :, :], typ[:, :, :], ALU.mult), low(6))
                    link(ve.tensor_reduce(e1[:, :], sc[:, :, :], AX.X, ALU.add), low(8))
                    link(ve.scalar_tensor_tensor(e2[:, :], e1[:, :], 0.2, e1[:, :], ALU.mult, ALU.max), low(10))
                    link(ve.tensor_copy(mb[:, 0:1], mb[:, K:K + 1]), low(12))
                    link(ve.tensor_tensor_scan(mb[:, 1:K + 1], cut[:, cc], e2[:, :], mb[:, 0:1], ALU.add, ALU.max), high(0))
                    link(ve.tensor_tensor(dl[:, 0, :], mb[:, 0:K], mb[:, 1:K + 1], ALU.subtract), high(1))
                    link(ve.tensor_tensor(dl[:, 0, :], dl[:, 0, :], cut[:, cc], ALU.add))
                    ve.tensor_tensor(dl[:, 1, :], e2[:, :], mb[:, 1:K + 1], ALU.subtract).then_inc(s_dl, 1)
                    link(ve.tensor_copy(XI[:, :, 0], S[:, :, K]), high(2))
                    if more:
                        highs(j + 1, range(3, K))
                    dve.wait_ge(s_ex, x0 + j + 1)
                    link(ve.tensor_tensor(XI[:, :, 1:K + 1], Tl[:, :, 0:CO].rearrange("p k c -> p c k"),
                                          ex[:, 1:2, :].to_broadcast([P, CO, K]), ALU.mult))
                    link(ve.tensor_tensor_scan(S[:, :, :].rearrange("p c k -> p (c k)"), decay[:, :, :].rearrange("p c k -> p (c k)"),
                                               XI[:, :, :].rearrange("p c k -> p (c k)"), 0.0, ALU.mult, ALU.add))
                    link(ve.reciprocal(rd[:, :], S[:, C, 1:K + 1]))
                    if not (static and i == 0):
                        if h == 0:
                            dve.wait_ge(s_dump[b], 32 * i)
                        else:
                            dve.wait_ge(s_wr[b], 16 * K * i)

                    def capture():
                        if h == 0 and not (static and b == 0):
                            keep_A(j - 1, 1 - b)
                        fe = first_end[:, cc]
                        link(ve.tensor_tensor(cap[:, :, :], SM[:, :, 1:K + 1], fe.unsqueeze(1).to_broadcast([P, CO + 1, K]), ALU.mult))
                        link(ve.tensor_reduce(part[:, :], cap[:, :, :], AX.X, ALU.add))
                        link(ve.tensor_tensor(first[:, :], first[:, :], part[:, :], ALU.add))

                    def free():
                        if ahead:
                            if h == 0:
                                dve.wait_ge(s_xc, j + 1)
                            indices(j + 2, b, h)

                    finish(h, K, b, H, r0 + j * nr, j + 1, S[:, 0:C, 1:K + 1].rearrange("p c k -> p k c"),
                           (capture, (lambda: take_rows(j + 1)) if more else nothing), free)
                    if h == 1:
                        ve.tensor_copy(place[:, b, :], write_f[:, cc]).then_inc(s_row, 1)

                def pair(i, static, h=h, chunk=chunk):
                    link.enter(i, 2 * PER[h])
                    chunk(i * 2, 0, static, True, i)
                    chunk(i * 2 + 1, 1, static, True, i)
                link.base += link.n
                steps(dve, pair, NP2 - 1)
                link.leave(NP2 - 1)
                chunk(NCH - 2, 0, False, False, NP2 - 1)
                chunk(NCH - 1, 1, False, False, NP2 - 1, False)

                ve.tensor_scalar(dg[:, 0, :], ident[:, :], mL, None, ALU.mult).then_inc(s_mat, 1)
                dve.wait_ge(s_bc, 6 + 3 * h + 1)
                if h == 0:
                    keep_A(NCH - 1, 1)
                link(ve.tensor_tensor(mm[:, :], earlier, psM[:, 0:P], ALU.mult))
                link(ve.tensor_tensor(mm[:, :], mm[:, :], not_earlier, ALU.add))
                link(ve.tensor_reduce(sv[:, 2:3], mm[:, :], AX.X, ALU.max))
                link(ve.tensor_tensor(sv[:, 2:3], sv[:, 2:3], mF, ALU.max))
                link(ve.tensor_tensor(sv[:, 3:4], mF, sv[:, 2:3], ALU.subtract))
                ve.tensor_scalar(sv[:, 2:3], sv[:, 2:3], -1.0, None, ALU.mult).then_inc(s_dl, 1)
                if h == 0:
                    dve.wait_ge(s_kept, NCH)
                    spread_A(0, 2)
                dve.wait_ge(s_bc, 6 + 3 * h + 2)
                ve.tensor_copy(sxT[:, :], psM[:, P:2 * P]).then_inc(s_mat, 1)
                if h == 0:
                    spread_A(2, 3)
                dve.wait_ge(s_ex, x0 + NCH + 1)
                link(ve.tensor_scalar(first[:, 0:CO], first[:, 0:CO], sv[:, 4:5], None, ALU.mult))
                dve.wait_ge(s_bc, 6 + 3 * h + 3)
                link(ve.tensor_tensor(first[:, 0:CO], first[:, 0:CO], psR[0][:, 0:CO], ALU.add))
                link(ve.tensor_scalar(first[:, C:CO], first[:, C:CO], 1e-30, None, ALU.max))
                link(ve.reciprocal(rd[:, 0:1], first[:, C:CO]))
                dve.wait_ge(s_sg, 16 + 16 * h)
                if h == 0:
                    dve.wait_ge(s_dump[0], 32 * NP2)
                else:
                    dve.wait_ge(s_wr[0], 16 * K * NP2)
                finish(h, 1, 0, seam_row.unsqueeze(1), r0 + NCH * nr, NCH + 1, first[:, 0:C].unsqueeze(1),
                       ((lambda: spread_A(3, 5), lambda: spread_A(5, 8)) if h == 0 else (nothing, nothing)), nothing)
                if h == 1:
                    ve.tensor_copy(capm[:, 0:1], rs[:, 0:1]).then_inc(s_si, 1)
                    break
                dve.wait_ge(s_xc, NCH + 1)
                ve.tensor_copy(first_A, rowO[:, 0, 0, A0:A0 + R]).then_inc(s_si, 1)
                indices(0, 0, 1)
                indices(1, 1, 1)
                spread_A(8, R)
                dve.wait_ge(s_lr, 16)
                dve.wait_ge(s_spread, R)
                dve.wait_ge(s_si, 2)


_INS = ['x', 'src', 'dst', 'edge_type_20', 'L0_gnn_relation_emb', 'L0_gnn_fc_w', 'L0_gnn_fc_b']


def kernel(**inputs):
    import numpy as _np
    import concourse.bacc as _bacc
    from concourse import mybir as _mybir
    from concourse.bass_utils import run_bass_kernel_spmd as _run

    nc = _bacc.Bacc("TRN2", target_bir_lowering=False, num_devices=1)
    arrays, args = {}, []
    for name in _INS:
        a = _np.ascontiguousarray(inputs[name])
        arrays[f"in_{name}"] = a
        args.append(nc.dram_tensor(f"in_{name}", a.shape, _mybir.dt.from_np(a.dtype), kind="ExternalInput").ap())
    out = nc.dram_tensor("out_0", inputs['x'].shape, _mybir.dt.float32, kind="ExternalOutput").ap()
    build_gnn(nc, *args, out)
    r = _run(nc, [arrays], core_ids=[0])
    return r.results[0]["out_0"]
```
